# Optimizing a Trainium2 kernel written in Bass

```python
import numpy as np
import jax
import jax.numpy as jnp

def _softmax(x, axis=-1):
    return jax.nn.softmax(x, axis=axis)

def _gelu(x):
    return jax.nn.gelu(x, approximate=True)

def _silu(x):
    return jax.nn.silu(x)

def _sigmoid(x):
    return jax.nn.sigmoid(x)

def _layernorm(x, axis=-1, eps=1e-05):
    m = jnp.mean(x, axis=axis, keepdims=True)
    v = jnp.var(x, axis=axis, keepdims=True)
    return (x - m) / jnp.sqrt(v + eps)

def _scatter_add(tgt, idx, src, axis=0):
    return tgt.at[idx].add(src)

def _segment_sum(src, seg, n):
    return jax.ops.segment_sum(src, seg, n)
kernel_name = 'mk_prb_d1_jaxref_r4_c2229c'

def setup_inputs(seed: int=0):
    np.random.seed(seed)
    _w = jnp.asarray

    def _L0_attn_setup():
        import jax, jax.numpy as jnp
        import numpy as np
        B, S, D = (4, 1024, 512)
        IDENTITY_WEIGHT = 0.5
        ROT_DIM = D // 2

        def _layernorm(x, gamma, beta, eps=1e-05):
            mu = jnp.mean(x, axis=-1, keepdims=True)
            var = jnp.var(x, axis=-1, keepdims=True)
            return (x - mu) * jax.lax.rsqrt(var + eps) * gamma + beta

        def _rotary(t, rot_dim, theta=10000.0):
            seq = t.shape[-2]
            inv_freq = 1.0 / theta ** (jnp.arange(0, rot_dim, 2, dtype=jnp.float32) / rot_dim)
            freqs = jnp.arange(seq, dtype=jnp.float32)[:, None] * inv_freq[None, :]
            freqs = jnp.repeat(freqs, 2, axis=-1)
            cos, sin = (jnp.cos(freqs), jnp.sin(freqs))
            t_rot, t_pass = (t[..., :rot_dim], t[..., rot_dim:])
            x1, x2 = (t_rot[..., 0::2], t_rot[..., 1::2])
            rot_half = jnp.stack([-x2, x1], axis=-1).reshape(t_rot.shape)
            return jnp.concatenate([t_rot * cos + rot_half * sin, t_pass], axis=-1)

        def _cos_sim(x):
            return x / jnp.linalg.norm(x, axis=-1, keepdims=True)
        key = jax.random.key(seed)
        ks = jax.random.split(key, 3)
        scale = 0.02
        return {'X': jax.random.normal(ks[0], (B, S, D), jnp.float32), 'W_in': jax.random.normal(ks[1], (D, 3 * D), jnp.float32) * scale, 'b_in': jnp.zeros((3 * D,), jnp.float32), 'W_out': jax.random.normal(ks[2], (D, D), jnp.float32) * scale, 'b_out': jnp.zeros((D,), jnp.float32), 'gamma': jnp.ones((D,), jnp.float32), 'beta': jnp.zeros((D,), jnp.float32)}
    _L0_attn_in = _L0_attn_setup()

    def _L0_ffn_setup():
        import jax, jax.numpy as jnp
        import numpy as np

        @jax.custom_vjp
        def ste_sign(x):
            return jnp.sign(x)

        def _ste_fwd(x):
            return (jnp.sign(x), None)

        def _ste_bwd(_, g):
            return (g,)
        ste_sign.defvjp(_ste_fwd, _ste_bwd)
        D_MODEL = 512
        D_HIDDEN = 2048
        key = jax.random.key(seed)
        k_x, k_up, k_dn = jax.random.split(key, 3)
        x = jax.random.normal(k_x, (2, 512, D_MODEL), dtype=jnp.float32)
        up_weight = jax.random.normal(k_up, (D_HIDDEN, D_MODEL), dtype=jnp.float32) * 0.02
        down_weight = jax.random.normal(k_dn, (D_MODEL, D_HIDDEN), dtype=jnp.float32) * 0.02
        up_scale = jnp.ones((D_HIDDEN,), dtype=jnp.float32)
        down_scale = jnp.ones((D_MODEL,), dtype=jnp.float32)
        output_scale = jnp.ones((1,), dtype=jnp.float32)
        return {'x': x, 'up_weight': up_weight, 'down_weight': down_weight, 'up_scale': up_scale, 'down_scale': down_scale, 'output_scale': output_scale}
    _L0_ffn_in = _L0_ffn_setup()
    _d = {'L0_attn_X': _L0_attn_in['X'], 'L0_attn_W_in': _L0_attn_in['W_in'], 'L0_attn_b_in': _L0_attn_in['b_in'], 'L0_attn_W_out': _L0_attn_in['W_out'], 'L0_attn_b_out': _L0_attn_in['b_out'], 'L0_attn_gamma': _L0_attn_in['gamma'], 'L0_attn_beta': _L0_attn_in['beta'], 'L0_ffn_up_weight': _L0_ffn_in['up_weight'], 'L0_ffn_down_weight': _L0_ffn_in['down_weight'], 'L0_ffn_up_scale': _L0_ffn_in['up_scale'], 'L0_ffn_down_scale': _L0_ffn_in['down_scale'], 'L0_ffn_output_scale': _L0_ffn_in['output_scale']}
    _x0 = _d['L0_attn_X']
    _d['L0_attn_X'] = jax.random.normal(jax.random.fold_in(jax.random.key(seed), 1), (8, 512, 512), dtype=_x0.dtype)
    del _x0
    return _d

def reference(L0_attn_X, L0_attn_W_in, L0_attn_b_in, L0_attn_W_out, L0_attn_b_out, L0_attn_gamma, L0_attn_beta, L0_ffn_up_weight, L0_ffn_down_weight, L0_ffn_up_scale, L0_ffn_down_scale, L0_ffn_output_scale):

    def _L0_attn_ref(X, W_in, b_in, W_out, b_out, gamma, beta):
        import jax, jax.numpy as jnp
        import numpy as np
        B, S, D = (4, 1024, 512)
        IDENTITY_WEIGHT = 0.5
        ROT_DIM = D // 2

        def _layernorm(x, gamma, beta, eps=1e-05):
            mu = jnp.mean(x, axis=-1, keepdims=True)
            var = jnp.var(x, axis=-1, keepdims=True)
            return (x - mu) * jax.lax.rsqrt(var + eps) * gamma + beta

        def _rotary(t, rot_dim, theta=10000.0):
            seq = t.shape[-2]
            inv_freq = 1.0 / theta ** (jnp.arange(0, rot_dim, 2, dtype=jnp.float32) / rot_dim)
            freqs = jnp.arange(seq, dtype=jnp.float32)[:, None] * inv_freq[None, :]
            freqs = jnp.repeat(freqs, 2, axis=-1)
            cos, sin = (jnp.cos(freqs), jnp.sin(freqs))
            t_rot, t_pass = (t[..., :rot_dim], t[..., rot_dim:])
            x1, x2 = (t_rot[..., 0::2], t_rot[..., 1::2])
            rot_half = jnp.stack([-x2, x1], axis=-1).reshape(t_rot.shape)
            return jnp.concatenate([t_rot * cos + rot_half * sin, t_pass], axis=-1)

        def _cos_sim(x):
            return x / jnp.linalg.norm(x, axis=-1, keepdims=True)
        Xn = _layernorm(X, gamma, beta)
        QKV = Xn @ W_in + b_in
        Q, K, V = jnp.split(QKV, 3, axis=-1)
        K = _rotary(K, ROT_DIM)
        V = _rotary(V, ROT_DIM)
        A = jnp.sum(_cos_sim(K) * _cos_sim(V), axis=-2)
        A = (1.0 - IDENTITY_WEIGHT) * A + IDENTITY_WEIGHT
        Y = A[:, None, :] * Q
        Y = Y @ W_out + b_out
        return Y + X

    def _L0_ffn_ref(x, up_weight, down_weight, up_scale, down_scale, output_scale):
        import jax, jax.numpy as jnp
        import numpy as np

        @jax.custom_vjp
        def ste_sign(x):
            return jnp.sign(x)

        def _ste_fwd(x):
            return (jnp.sign(x), None)

        def _ste_bwd(_, g):
            return (g,)
        ste_sign.defvjp(_ste_fwd, _ste_bwd)
        D_MODEL = 512
        D_HIDDEN = 2048
        up_w = ste_sign(up_weight)
        down_w = ste_sign(down_weight)
        hidden = jnp.einsum('bsd,hd->bsh', x, up_w) * up_scale
        hidden = jax.nn.relu(hidden)
        out = jnp.einsum('bsh,dh->bsd', hidden, down_w) * down_scale
        return out * output_scale
    x = L0_attn_X
    xn = _layernorm(x, axis=-1)
    x = x + _L0_attn_ref(xn, L0_attn_W_in, L0_attn_b_in, L0_attn_W_out, L0_attn_b_out, L0_attn_gamma, L0_attn_beta) + _L0_ffn_ref(xn, L0_ffn_up_weight, L0_ffn_down_weight, L0_ffn_up_scale, L0_ffn_down_scale, L0_ffn_output_scale)
    return x

_drawn_inputs = setup_inputs


def setup_inputs(seed=0):
    import zlib

    import numpy as np

    out = dict(_drawn_inputs(seed))
    spreads = {'L0_attn_b_in': (0.0, 2.0),
     'L0_attn_b_out': (0.0, 2.0),
     'L0_attn_gamma': (1.0, 0.6),
     'L0_attn_beta': (0.0, 2.0),
     'L0_ffn_up_scale': (1.0, 0.2),
     'L0_ffn_down_scale': (1.0, 0.2)}
    factors = {'L0_attn_W_in': 36.163, 'L0_attn_W_out': 35.807}
    for name, (base, spread) in spreads.items():
        noise = np.random.default_rng([zlib.crc32(name.encode()), seed]).standard_normal(out[name].shape)
        drawn = base * np.exp(spread * noise) if base else spread * noise
        out[name] = jnp.asarray(drawn.astype(out[name].dtype))
    for name, factor in factors.items():
        out[name] = (out[name] * factor).astype(out[name].dtype)
    return out
```

```python
from contextlib import ExitStack

import numpy as np
import concourse.bass as bass
from concourse import mybir

P = 128
F32 = mybir.dt.float32
F32R = mybir.dt.float32r
BF16 = mybir.dt.bfloat16
ALU = mybir.AluOpType
ACT = mybir.ActivationFunctionType
EPS = 1e-5
THETA = 10000.0

SIGN_SLOTS = 4
HID_SLOTS = 4
FULL_SLOTS = 2
UP_BANKS = 3
DOWN_LAG = 2


def attention_ffn_kernel(nc, x, w_in, w_out, up, down, gamma, beta, b_kv, b_q, b_out, up_scale, down_scale,
                         output_scale, rotation, identity, out):
    NB, SEQ, D = x.shape
    R = SEQ // P
    K = D // P
    H = up.shape[0]
    HALF = D // 4
    assert SEQ == 512 and D == 512 and R == 4 and K == 4 and H > 8

    ctx = ExitStack()
    with ctx:
        def sb(name, shape, dt=F32):
            return ctx.enter_context(nc.sbuf_tensor(name, shape, dt))

        def sem(name):
            return ctx.enter_context(nc.semaphore(name))

        win_hi = sb("win_hi", [P, 3, K, D], F32R)
        win_lo = sb("win_lo", [P, 3, K, D], F32R)
        wout_hi = sb("wout_hi", [P, K, D], F32R)
        wout_lo = sb("wout_lo", [P, K, D], F32R)
        up_sign = sb("up_sign", [P, H, K, P], F32R)
        down_sign = sb("down_sign", [P, H, D], F32R)
        xz = sb("xz", [P, R, D])
        res = sb("res", [P, R, D])
        zt_hi = sb("zt_hi", [P, K, SEQ], F32R)
        zt_lo = sb("zt_lo", [P, K, SEQ], F32R)
        hid_hi = sb("hid_hi", [P, HID_SLOTS, SEQ], F32R)
        hid_lo = sb("hid_lo", [P, HID_SLOTS, SEQ], F32R)
        full = sb("full", [P, FULL_SLOTS, SEQ])
        kb = sb("kb", [P, D])
        vb = sb("vb", [P, D])
        prod = sb("prod", [P, 6, HALF])
        acc_p = sb("acc_p", [P, 4, HALF])
        acc_r = sb("acc_r", [P, 4, HALF])
        junk = sb("junk", [P, D], BF16)
        rot = sb("rot", [P, R, 2, HALF])
        bias_kv = sb("bias_kv", [P, 2, D])
        bout_bc = sb("bout_bc", [P, D])
        dscale_bc = sb("dscale_bc", [P, D])
        ident = sb("ident", [P, P])
        gamma_c = sb("gamma_c", [P, K])
        beta_c = sb("beta_c", [P, K])
        bq_c = sb("bq_c", [P, K])
        uscale_c = sb("uscale_c", [P, H])
        oscale_c = sb("oscale_c", [P, 1])
        half_c = sb("half_c", [P, 2])
        bn = sb("bn", [P, R, 6])
        st = sb("st", [P, 8, R])
        root = sb("root", [P, 2, R])
        inv = sb("inv", [P, 2, R])
        nxt = sb("nxt", [P, 3, R])
        cur = sb("cur", [P, 3, R])
        nsq = sb("nsq", [P, R, 2])
        nrm = sb("nrm", [P, R, 2])
        nw = sb("nw", [P, 3, 2])
        wrow = sb("wrow", [P, 1])
        comb = sb("comb", [P, 6, HALF]) if False else prod
        acol = sb("acol", [P, 2, K])

        banks = [ctx.enter_context(nc.psum_tensor(f"bank{i}", [P, 512], F32)) for i in range(8)]

        small_in = sem("small_in")
        x0_in = [sem(f"x0_in{r}") for r in range(R)]
        x_in = sem("x_in")
        res_in = sem("res_in")
        piece_in = [sem(f"piece_in{i}") for i in range(K)]
        sign_in = [sem(f"sign_in{i}") for i in range(SIGN_SLOTS)]
        out_dma = sem("out_dma")
        consts_set = sem("consts_set")
        piece_hi = sem("piece_hi")
        piece_lo = sem("piece_lo")
        beta_mm = sem("beta_mm")
        bias_kv_set = sem("bias_kv_set")
        betaq_mm = sem("betaq_mm")
        bq_set = sem("bq_set")
        wq_set = sem("wq_set")
        wout_set = sem("wout_set")
        pool_step = sem("pool_step")
        up_signed = sem("up_signed")
        down_signed = sem("down_signed")
        kv_mm = sem("kv_mm")
        up_mm = sem("up_mm")
        down_mm = sem("down_mm")
        a_mm = sem("a_mm")
        q_mm = sem("q_mm")
        t_mm = sem("t_mm")
        y_mm = sem("y_mm")
        squared = sem("squared")
        normed = sem("normed")
        relu_set = sem("relu_set")
        root_set = sem("root_set")
        q_set = sem("q_set")
        zt_hi_set = sem("zt_hi_set")
        kv_biased = sem("kv_biased")
        hid_set = sem("hid_set")
        acc_set = sem("acc_set")
        a_set = sem("a_set")
        roots_due = sem("roots_due")
        z_set = sem("z_set")
        ffn_read = sem("ffn_read")
        res_set = sem("res_set")
        q_split = sem("q_split")
        zt_set = sem("zt_set")
        out_set = sem("out_set")
        dve_step = sem("dve_step")

        block = ctx.enter_context(nc.Block())
        LAST = NB - 1

        @block.sync
        def _(sp):
            def small(dst, src):
                sp.dma_start(dst, src).then_inc(small_in, 16)

            for r in range(R):
                sp.dma_start(xz[:, r, :], x[0, r * P:(r + 1) * P, :]).then_inc(x0_in[r], 16)
                if r == 0:
                    small(gamma_c[:], gamma)
                    small(beta_c[:], beta)
                    small(ident[:], identity)
            for n in range(2 * K):
                if n >= K:
                    sp.wait_ge(piece_hi, n - K + 1)
                    sp.wait_ge(piece_lo, n - K + 1)
                    sp.wait_ge(beta_mm, n - K + 1)
                sp.dma_start(res[:, n % K, :], w_in[n // K, n % K]).then_inc(piece_in[n % K], 16)
                if n == K - 1:
                    small(bias_kv[:].rearrange("p a d -> p (a d)"), b_kv.partition_broadcast(P))
                    small(rot[:], rotation)
                    small(uscale_c[:], up_scale)
                    small(bq_c[:], b_q)
                    small(bout_bc[:], b_out.partition_broadcast(P))
                    small(dscale_bc[:], down_scale.partition_broadcast(P))
                    small(oscale_c[:], output_scale.partition_broadcast(P))

            def sign_piece(n):
                if n < SIGN_SLOTS:
                    sp.wait_ge(t_mm, K)
                elif n % 2 == 0:
                    sp.wait_ge(up_signed, (n - SIGN_SLOTS) // 2 + 1)
                else:
                    sp.wait_ge(down_signed, (n - SIGN_SLOTS) // 2 + 1)
                src = (up if n % 2 == 0 else down)[n // 2]
                sp.dma_start(xz[:, n % SIGN_SLOTS, :], src).then_inc(sign_in[n % SIGN_SLOTS], 16)

            def late_piece(n):
                if n < K:
                    sp.wait_ge(piece_hi, K + n + 1)
                    sp.wait_ge(piece_lo, K + n + 1)
                    sp.wait_ge(beta_mm, K + n + 1)
                else:
                    sp.wait_ge(wq_set, n - K + 1)
                src = w_in[2, n] if n < K else w_out[n - K]
                sp.dma_start(res[:, n % K, :], src).then_inc(piece_in[n % K], 16)

            for n in range(SIGN_SLOTS):
                sign_piece(n)
            for n in range(K):
                late_piece(n)
            for n in range(SIGN_SLOTS, 2 * H):
                sign_piece(n)
                if 2 * K <= n < 4 * K and n % 2 == 0:
                    late_piece(K + (n - 2 * K) // 2)

            def sequence(b, first, last):
                if first:
                    sp.wait_ge(wout_set, K)
                else:
                    sp.wait_ge(out_dma, b * (16 * R))
                sp.dma_start(res[:], x[b].rearrange("(r p) d -> p r d", p=P)).then_inc(res_in, 16)
                if not last:
                    if first:
                        sp.wait_ge(up_signed, H)
                        sp.wait_ge(down_signed, H)
                    else:
                        sp.wait_ge(t_mm, b * K + K)
                    sp.dma_start(xz[:], x[b + 1].rearrange("(r p) d -> p r d", p=P)).then_inc(x_in, 16)
                for r in range(R):
                    sp.wait_ge(out_set, b * R + (r + 1))
                    sp.dma_start(out[b].rearrange("(r p) d -> r p d", p=P)[r], res[:, r, :]).then_inc(out_dma, 16)

            sequence(0, True, False)
            with sp.Fori(1, LAST) as b:
                sequence(b, False, False)
            sequence(LAST, False, True)
            sp.wait_ge(out_dma, NB * R * 16)

        @block.gpsimd
        def _(pool):
            done = 0
            for n in range(2 * K):
                raw = res[:, n % K, :]
                hi = win_hi[:, 2, n, :] if n < K else wout_hi[:, n - K, :]
                lo = win_lo[:, 2, n, :] if n < K else wout_lo[:, n - K, :]
                pool.wait_ge(small_in, 3 * 16)
                pool.wait_ge(piece_in[n % K], 16 * (3 + n // K))
                if n < K:
                    pool.wait_ge(betaq_mm, n + 1)
                    nc.gpsimd.tensor_scalar(raw, raw, gamma_c[:, n:n + 1], None, ALU.mult).then_inc(pool_step, 1)
                    done += 1
                    pool.wait_ge(pool_step, done)
                nc.gpsimd.tensor_copy(hi, raw).then_inc(pool_step, 1)
                done += 1
                pool.wait_ge(pool_step, done)
                nc.gpsimd.tensor_tensor(lo, raw, hi.bitcast(F32), ALU.subtract).then_inc(wq_set if n < K else wout_set, 1)

        @block.scalar
        def _(act):
            def piece(n):
                act.wait_ge(piece_in[n % K], 16 * (n // K + 1))
                nc.scalar.activation(win_hi[:, n // K, n % K, :], res[:, n % K, :], ACT.Copy,
                                     scale=gamma_c[:, n % K:n % K + 1]).then_inc(piece_hi, 1)

            def sign_up(c):
                n = 2 * c
                act.wait_ge(sign_in[n % SIGN_SLOTS], 16 * (n // SIGN_SLOTS + 1))
                nc.scalar.activation(up_sign[:, c].rearrange("p k h -> p (k h)"), xz[:, n % SIGN_SLOTS, :],
                                     ACT.Sign).then_inc(up_signed, 1)

            def sign_down(c):
                n = 2 * c + 1
                act.wait_ge(sign_in[n % SIGN_SLOTS], 16 * (n // SIGN_SLOTS + 1))
                nc.scalar.activation(down_sign[:, c, :], xz[:, n % SIGN_SLOTS, :], ACT.Sign).then_inc(down_signed, 1)

            def roots(b):
                act.wait_ge(roots_due, b + 1)
                nc.scalar.activation(root[:], st[:, 0:2, :], ACT.Sqrt).then_inc(root_set, 1)

            def transposed_hi(b, k):
                act.wait_ge(t_mm, b * K + (k + 1))
                nc.scalar.activation(zt_hi[:, k, :], banks[k][:], ACT.Copy).then_inc(zt_hi_set, 1)

            def norms(b, r):
                for j, src in enumerate((kb, vb)):
                    act.wait_ge(kv_biased, b * (2 * R) + (2 * r + j + 1))
                    if r + j:
                        act.wait_ge(squared, b * (2 * R) + (2 * r + j))
                    nc.scalar.activation(junk[:], src[:], ACT.Square, accum_out=nsq[:, r, j:j + 1]).then_inc(squared, 1)
                act.wait_ge(squared, b * (2 * R) + (2 * r + 2))
                nc.scalar.activation(nrm[:, r, :], nsq[:, r, :], ACT.Sqrt).then_inc(normed, 1)

            def relu(b, c):
                bank = banks[4 + c % UP_BANKS]
                act.wait_ge(up_mm, b * H + (c + 1))
                if c >= HID_SLOTS:
                    act.wait_ge(down_mm, b * H + (c - HID_SLOTS + 1))
                if c >= FULL_SLOTS:
                    act.wait_ge(hid_set, b * H + (c - FULL_SLOTS + 1))
                nc.scalar.activation(full[:, c % FULL_SLOTS, :], bank[:], ACT.Relu, scale=uscale_c[:, c:c + 1])
                nc.scalar.activation(hid_hi[:, c % HID_SLOTS, :], bank[:], ACT.Relu,
                                     scale=uscale_c[:, c:c + 1]).then_inc(relu_set, 1)

            def scaled_q(b, q):
                act.wait_ge(q_mm, b * K + (q + 1))
                if q == 0:
                    act.wait_ge(a_set, b + 1)
                    act.wait_ge(hid_set, b * H + H)
                    act.wait_ge(down_mm, b * H + H)
                if q >= FULL_SLOTS:
                    act.wait_ge(q_split, b * K + (q - FULL_SLOTS + 1))
                for dst in (full[:, q % FULL_SLOTS, :], hid_hi[:, q, :]):
                    last = nc.scalar.activation(dst, banks[4 + q][:], ACT.Identity, scale=acol[:, 0, q:q + 1],
                                                bias=acol[:, 1, q:q + 1])
                last.then_inc(q_set, 1)

            def sequence(b, first, last):
                for r in range(R):
                    norms(b, r)
                    if first:
                        if r < SIGN_SLOTS // 2:
                            sign_up(r)
                            sign_down(r)
                for c in range(H):
                    relu(b, c)
                    if first and c + SIGN_SLOTS // 2 < H:
                        sign_up(c + SIGN_SLOTS // 2)
                        sign_down(c + SIGN_SLOTS // 2)
                    if not last and not first and c == 10:
                        roots(b + 1)
                for q in range(K):
                    scaled_q(b, q)
                    if first and q == 2:
                        roots(b + 1)
                if not last:
                    for k in range(K):
                        transposed_hi(b + 1, k)

            act.wait_ge(small_in, 3 * 16)
            roots(0)
            for n in range(K):
                piece(n)
            for k in range(K):
                transposed_hi(0, k)
            for n in range(K, 2 * K):
                piece(n)
            act.wait_ge(small_in, 10 * 16)
            sequence(0, True, False)
            with act.Fori(1, LAST) as b:
                sequence(b, False, False)
            sequence(LAST, False, True)

        @block.vector
        def _(dve):
            count = [0]

            def step(ins):
                count[0] += 1
                ins.then_inc(dve_step, 1)
                return count[0]

            def landed(base, n):
                dve.wait_ge(dve_step, base + n)

            def link(base, ins):
                landed(base, step(ins))

            def newton_rsqrt(base, y, a, t):
                link(base, nc.vector.scalar_tensor_tensor(out=t, in0=y, scalar=-0.5, in1=y, op0=ALU.mult, op1=ALU.mult))
                link(base, nc.vector.tensor_tensor(t, t, a, ALU.mult))
                link(base, nc.vector.scalar_tensor_tensor(out=y, in0=t, scalar=1.5, in1=y, op0=ALU.add, op1=ALU.mult))

            def row_stats(r):
                return nc.vector.bn_stats(bn[:, r, :], xz[:, r, :])

            def moments(base):
                S = st
                step(nc.vector.tensor_tensor(S[:, 2, :], bn[:, :, 1], bn[:, :, 4], ALU.add))
                step(nc.vector.tensor_tensor(S[:, 3, :], bn[:, :, 1], bn[:, :, 4], ALU.subtract))
                link(base, nc.vector.tensor_tensor(S[:, 4, :], bn[:, :, 2], bn[:, :, 5], ALU.add))
                step(nc.vector.tensor_scalar(nxt[:, 0, :], S[:, 2, :], 0.5, None, ALU.mult))
                link(base, nc.vector.scalar_tensor_tensor(out=S[:, 5, :], in0=S[:, 3, :], scalar=0.25, in1=S[:, 3, :],
                                                          op0=ALU.mult, op1=ALU.mult))
                link(base, nc.vector.scalar_tensor_tensor(out=S[:, 6, :], in0=S[:, 4, :], scalar=1.0 / D, in1=S[:, 5, :],
                                                          op0=ALU.mult, op1=ALU.add))
                link(base, nc.vector.tensor_scalar(S[:, 0, :], S[:, 6, :], EPS, None, ALU.add))
                nc.vector.scalar_tensor_tensor(out=S[:, 1, :], in0=S[:, 0, :], scalar=EPS, in1=S[:, 6, :],
                                               op0=ALU.mult, op1=ALU.add).then_inc(roots_due, 1)

            def scales(base, b):
                dve.wait_ge(root_set, b + 1)
                link(base, nc.vector.reciprocal(inv[:], root[:]))
                newton_rsqrt(base, inv[:], st[:, 0:2, :], st[:, 2:4, :])
                step(nc.vector.tensor_scalar(nxt[:, 1, :], inv[:, 0, :], 1.0, None, ALU.add))
                link(base, nc.vector.tensor_tensor(st[:, 4, :], st[:, 1, :], inv[:, 1, :], ALU.mult))
                link(base, nc.vector.tensor_tensor(nxt[:, 2, :], st[:, 4, :], inv[:, 0, :], ALU.mult))

            def normalise(r):
                nc.vector.tensor_scalar(xz[:, r, :], xz[:, r, :], nxt[:, 0, r:r + 1], inv[:, 1, r:r + 1],
                                        ALU.subtract, ALU.mult).then_inc(z_set, 1)

            def transposed_lo(b, k):
                dve.wait_ge(zt_hi_set, b * K + (k + 1))
                nc.vector.tensor_tensor(zt_lo[:, k, :], banks[k][:], zt_hi[:, k, :].bitcast(F32),
                                        ALU.subtract).then_inc(zt_set, 1)

            def piece(n):
                dve.wait_ge(piece_hi, n + 1)
                nc.vector.scalar_tensor_tensor(out=win_lo[:, n // K, n % K, :], in0=res[:, n % K, :],
                                               scalar=gamma_c[:, n % K:n % K + 1],
                                               in1=win_hi[:, n // K, n % K, :].bitcast(F32),
                                               op0=ALU.mult, op1=ALU.subtract).then_inc(piece_lo, 1)

            def products(base, b, r):
                landed(base, count[0])
                for j, dst in enumerate((kb, vb)):
                    dve.wait_ge(kv_mm, b * (2 * R) + (2 * r + j + 1))
                    if r:
                        dve.wait_ge(squared, b * (2 * R) + (2 * (r - 1) + j + 1))
                    nc.vector.tensor_tensor(dst[:], banks[2 * (r % 2) + j][:], bias_kv[:, j, :],
                                            ALU.add).then_inc(kv_biased, 1)
                dve.wait_ge(kv_biased, b * (2 * R) + (2 * r + 2))
                nc.vector.tensor_tensor(prod[:, 2:6, :].rearrange("p a i -> p (a i)"), kb[:], vb[:], ALU.mult)
                nc.vector.tensor_tensor(prod[:, 0, :], kb[:, 0:HALF], vb[:, HALF:2 * HALF], ALU.mult)
                crossed = step(nc.vector.tensor_tensor(prod[:, 1, :], kb[:, HALF:2 * HALF], vb[:, 0:HALF], ALU.mult))
                landed(base, crossed)
                dve.wait_ge(squared, b * (2 * R) + (2 * r + 1))
                table = rot[:, r, :, :].unsqueeze(2).to_broadcast([P, 2, 2, HALF])
                step(nc.vector.tensor_tensor(kb[:].rearrange("p (a c i) -> p a c i", a=2, c=2),
                                             prod[:, 0:4, :].rearrange("p (a c) i -> p a c i", a=2), table, ALU.mult))

            def accumulate(base, b, r):
                dve.wait_ge(normed, b * R + (r + 1))
                y, t = nw[:, 0, :], nw[:, 1, :]
                link(base, nc.vector.reciprocal(y, nrm[:, r, :]))
                newton_rsqrt(base, y, nsq[:, r, :], t)
                link(base, nc.vector.tensor_tensor(wrow[:], nw[:, 0, 0:1], nw[:, 0, 1:2], ALU.mult))
                flat = "p a i -> p (a i)"
                for dst, src in ((acc_p, prod[:, 2:6, :].rearrange(flat)), (acc_r, kb[:])):
                    dst = dst[:].rearrange(flat)
                    if r == 0:
                        last = nc.vector.tensor_scalar(dst, src, wrow[:, 0:1], None, ALU.mult)
                    else:
                        last = nc.vector.scalar_tensor_tensor(out=dst, in0=src, scalar=wrow[:, 0:1], in1=dst,
                                                              op0=ALU.mult, op1=ALU.add)
                    step(last)

            def combine(base):
                landed(base, count[0])
                step(nc.vector.tensor_tensor(prod[:, 0, :], acc_p[:, 0, :], acc_p[:, 1, :], ALU.add))
                step(nc.vector.tensor_tensor(prod[:, 1, :], acc_r[:, 2, :], acc_r[:, 3, :], ALU.subtract))
                link(base, nc.vector.tensor_tensor(prod[:, 2, :], acc_r[:, 0, :], acc_r[:, 1, :], ALU.add))
                link(base, nc.vector.tensor_tensor(prod[:, 3, :], prod[:, 1, :], prod[:, 2, :], ALU.subtract))
                nc.vector.tensor_tensor(acc_p[:, 0, :], prod[:, 0, :], prod[:, 3, :], ALU.add)
                nc.vector.tensor_tensor(acc_p[:, 1, :], prod[:, 0, :], prod[:, 3, :], ALU.subtract).then_inc(acc_set, 1)

            def attention_scale(b):
                dve.wait_ge(a_mm, b + 1)
                nc.vector.tensor_scalar(acol[:, 0, :], banks[7][:, 0:K], 0.5, None, ALU.add).then_inc(dve_step, 1)
                count[0] += 1

            def attention_bias(base):
                landed(base, count[0])
                nc.vector.tensor_tensor(acol[:, 1, :], acol[:, 0, :], bq_c[:], ALU.mult).then_inc(a_set, 1)

            def hidden_lo(b, c):
                dve.wait_ge(relu_set, b * H + (c + 1))
                nc.vector.tensor_tensor(hid_lo[:, c % HID_SLOTS, :], full[:, c % FULL_SLOTS, :],
                                        hid_hi[:, c % HID_SLOTS, :].bitcast(F32), ALU.subtract).then_inc(hid_set, 1)

            def residual(base, b, r):
                if r == 0:
                    dve.wait_ge(res_in, b * 16 + 16)
                link(base, nc.vector.tensor_scalar(res[:, r, :], res[:, r, :], cur[:, 0, r:r + 1], cur[:, 1, r:r + 1],
                                                   ALU.subtract, ALU.mult))
                step(nc.vector.tensor_tensor(res[:, r, :], res[:, r, :], bout_bc[:], ALU.add))

            def ffn_scaled(b, r):
                dve.wait_ge(down_mm, b * H + H)
                if r >= 2:
                    dve.wait_ge(res_set, b * R + (r - 1))
                nc.vector.scalar_tensor_tensor(out=(kb, vb)[r % 2][:], in0=banks[r][:], scalar=cur[:, 2, r:r + 1],
                                               in1=dscale_bc[:], op0=ALU.mult, op1=ALU.mult).then_inc(ffn_read, 1)

            def ffn_added(b, r):
                dve.wait_ge(ffn_read, b * R + (r + 1))
                nc.vector.scalar_tensor_tensor(out=res[:, r, :], in0=(kb, vb)[r % 2][:], scalar=cur[:, 0, r:r + 1],
                                               in1=res[:, r, :], op0=ALU.add, op1=ALU.add).then_inc(res_set, 1)

            def query_lo(b, q):
                dve.wait_ge(q_set, b * K + (q + 1))
                nc.vector.tensor_tensor(hid_lo[:, q, :], full[:, q % FULL_SLOTS, :], hid_hi[:, q, :].bitcast(F32),
                                        ALU.subtract).then_inc(q_split, 1)

            def finish(b, r):
                dve.wait_ge(y_mm, b * R + (r + 1))
                dve.wait_ge(res_set, b * R + (r + 1))
                nc.vector.tensor_tensor(res[:, r, :], banks[4 + r][:], res[:, r, :], ALU.add).then_inc(out_set, 1)

            def sequence(b, first, last, base):
                count[0] = 0
                step(nc.vector.tensor_copy(cur[:], nxt[:]))
                for r in range(R):
                    products(base, b, r)
                    accumulate(base, b, r)
                combine(base)
                for c in range(H):
                    hidden_lo(b, c)
                    if c == 3:
                        if first:
                            dve.wait_ge(betaq_mm, K)
                            nc.vector.tensor_tensor(bq_c[:], banks[7][:, 8:8 + K], bq_c[:], ALU.add).then_inc(bq_set, 1)
                            dve.wait_ge(bq_set, 1)
                        attention_scale(b)
                        attention_bias(base)
                    if not last and not first:
                        if 4 <= c < 4 + R:
                            if c == 4:
                                dve.wait_ge(x_in, b * 16 + 16)
                            step(row_stats(c - 4))
                        if c == 8:
                            landed(base, count[0])
                            moments(base)
                        if c == 10:
                            scales(base, b + 1)
                        if 11 <= c < 11 + R:
                            normalise(c - 11)
                    if c >= H - R and not first:
                        residual(base, b, c - (H - R))
                if first:
                    for r in range(R):
                        residual(base, b, r)
                landed(base, count[0])
                ffn_scaled(b, 0)
                ffn_scaled(b, 1)
                ffn_added(b, 0)
                ffn_added(b, 1)
                query_lo(b, 0)
                ffn_scaled(b, 2)
                ffn_scaled(b, 3)
                ffn_added(b, 2)
                ffn_added(b, 3)
                query_lo(b, 1)
                if first:
                    dve.wait_ge(x_in, 16)
                    for r in range(R):
                        step(row_stats(r))
                    landed(base, count[0])
                    moments(base)
                query_lo(b, 2)
                if first:
                    scales(base, b + 1)
                    for r in range(R):
                        normalise(r)
                query_lo(b, 3)
                if not last:
                    for k in range(K):
                        transposed_lo(b + 1, k)
                for r in range(R):
                    finish(b, r)
                return count[0]

            nc.vector.memset(half_c[:, 0:1], 0.25).then_inc(consts_set, 1)
            nc.vector.memset(half_c[:, 1:2], 0.5).then_inc(consts_set, 1)
            beta_bc = full[:, 0, :].rearrange("p (k j) -> p k j", k=K)
            link(0, nc.vector.memset(full[:, 0, :], 1.0))
            for r in range(R):
                dve.wait_ge(x0_in[r], 16)
                step(row_stats(r))
            dve.wait_ge(small_in, 3 * 16)
            for k in range(K):
                last = nc.vector.tensor_scalar(beta_bc[:, k, :], beta_bc[:, k, :], beta_c[:, k:k + 1], None, ALU.mult)
            last.then_inc(consts_set, 1)
            landed(0, count[0])
            moments(0)
            scales(0, 0)
            for r in range(R):
                normalise(r)
            for n in range(K):
                piece(n)
            for k in range(K):
                transposed_lo(0, k)
            for n in range(K, 2 * K):
                piece(n)
            dve.wait_ge(small_in, 10 * 16)
            step(nc.vector.tensor_scalar(dscale_bc[:], dscale_bc[:], oscale_c[:, 0:1], None, ALU.mult))
            for j in range(2):
                dve.wait_ge(beta_mm, K * (j + 1))
                nc.vector.tensor_tensor(bias_kv[:, j, :], banks[4 + j][:], bias_kv[:, j, :], ALU.add).then_inc(bias_kv_set, 1)
            dve.wait_ge(bias_kv_set, 2)
            start = count[0]
            n0 = sequence(0, True, False, start)
            with dve.Fori(1, LAST) as b:
                per = sequence_steps = [None]
                per = n0
                n = sequence(b, False, False, b * per + start)
                assert n == n0, (n, n0)
            sequence(LAST, False, True, LAST * n0 + start)

        @block.tensor
        def _(pe):
            mm = nc.tensor.matmul

            def three_pass(dst, l_hi, l_lo, r_hi, r_lo, k):
                mm(dst, l_hi, r_hi, start=(k == 0), stop=False)
                mm(dst, l_lo, r_hi, start=False, stop=False)
                return mm(dst, l_hi, r_lo, start=False, stop=(k == K - 1))

            def transposes(b, k):
                for r in range(R):
                    last = nc.tensor.transpose(banks[k][:, r * P:(r + 1) * P], xz[:, r, k * P:(k + 1) * P], ident[:])
                last.then_inc(t_mm, 1)

            def keys_values(b, r):
                for j in range(2):
                    bank = banks[2 * (r % 2) + j]
                    if r >= 2:
                        pe.wait_ge(kv_biased, b * (2 * R) + (2 * (r - 2) + j + 1))
                    for k in range(K):
                        s = slice(r * P, (r + 1) * P)
                        last = three_pass(bank[:], zt_hi[:, k, s], zt_lo[:, k, s], win_hi[:, j, k, :],
                                          win_lo[:, j, k, :], k)
                    last.then_inc(kv_mm, 1)

            def up_proj(b, c, first):
                bank = banks[4 + c % UP_BANKS]
                if c >= UP_BANKS:
                    pe.wait_ge(relu_set, b * H + (c - UP_BANKS + 1))
                if first:
                    pe.wait_ge(up_signed, c + 1)
                for k in range(K):
                    mm(bank[:], up_sign[:, c, k, :], zt_hi[:, k, :], start=(k == 0), stop=False)
                    last = mm(bank[:], up_sign[:, c, k, :], zt_lo[:, k, :], start=False, stop=(k == K - 1))
                last.then_inc(up_mm, 1)

            def down_proj(b, c, first):
                pe.wait_ge(hid_set, b * H + (c + 1))
                if first:
                    pe.wait_ge(down_signed, c + 1)
                for r in range(R):
                    s = slice(r * P, (r + 1) * P)
                    mm(banks[r][:], hid_hi[:, c % HID_SLOTS, s], down_sign[:, c, :], start=(c == 0), stop=False)
                    last = mm(banks[r][:], hid_lo[:, c % HID_SLOTS, s], down_sign[:, c, :], start=False,
                              stop=(c == H - 1))
                last.then_inc(down_mm, 1)

            def beta_query(n):
                pe.wait_ge(piece_in[n], 3 * 16)
                for q in range(K):
                    last = mm(banks[7][:, 8 + q:9 + q], res[:, n, q * P:(q + 1) * P], beta_c[:, n:n + 1],
                              start=(n == 0 and q == 0), stop=(n == K - 1), skip_group_check=True)
                last.then_inc(betaq_mm, 1)

            def row_sums(b):
                pe.wait_ge(acc_set, b + 1)
                for q in range(K):
                    last = mm(banks[7][:, q:q + 1], acc_p[:, q, :], half_c[:, q // 2:q // 2 + 1], start=True, stop=True)
                last.then_inc(a_mm, 1)

            def sequence(b, first, last):
                pe.wait_ge(zt_set, b * K + K)
                for r in range(R):
                    keys_values(b, r)
                if not first:
                    pe.wait_ge(out_set, b * R)
                for c in range(H + DOWN_LAG):
                    if c < H:
                        up_proj(b, c, first)
                    if c == DOWN_LAG:
                        pe.wait_ge(kv_biased, b * (2 * R) + 2 * R)
                    if c >= DOWN_LAG:
                        down_proj(b, c - DOWN_LAG, first)
                    if first and c == 2:
                        for n in range(K):
                            beta_query(n)
                    if c == 4:
                        if first:
                            pe.wait_ge(bq_set, 1)
                        row_sums(b)
                pe.wait_ge(relu_set, b * H + H)
                pe.wait_ge(a_set, b + 1)
                if first:
                    pe.wait_ge(wq_set, K)
                for q in range(K):
                    s = slice(q * P, (q + 1) * P)
                    for k in range(K):
                        done = three_pass(banks[4 + q][:], win_hi[:, 2, k, s], win_lo[:, 2, k, s], zt_hi[:, k, :],
                                          zt_lo[:, k, :], k)
                    done.then_inc(q_mm, 1)
                if not last:
                    pe.wait_ge(z_set, b * R + 2 * R)
                    for k in range(K):
                        pe.wait_ge(ffn_read, b * R + (k + 1))
                        transposes(b + 1, k)
                if first:
                    pe.wait_ge(wout_set, K)
                pe.wait_ge(q_split, b * K + K)
                for r in range(R):
                    s = slice(r * P, (r + 1) * P)
                    for k in range(K):
                        done = three_pass(banks[4 + r][:], hid_hi[:, k, s], hid_lo[:, k, s], wout_hi[:, k, :],
                                          wout_lo[:, k, :], k)
                    done.then_inc(y_mm, 1)

            pe.wait_ge(small_in, 3 * 16)
            pe.wait_ge(z_set, R)
            for k in range(K):
                transposes(0, k)
            pe.wait_ge(consts_set, 3)
            beta_bc = full[:, 0, :].rearrange("p (k j) -> p k j", k=K)
            for n in range(2 * K):
                pe.wait_ge(piece_in[n % K], 16 * (n // K + 1))
                mm(banks[4 + n // K][:], beta_bc[:, n % K, :], res[:, n % K, :], start=(n % K == 0),
                   stop=(n % K == K - 1)).then_inc(beta_mm, 1)
            pe.wait_ge(piece_lo, 2 * K)
            pe.wait_ge(bias_kv_set, 2)
            sequence(0, True, False)
            with pe.Fori(1, LAST) as b:
                sequence(b, False, False)
            sequence(LAST, False, True)


def kernel(**inputs):
    import numpy as _np
    import concourse.bacc as _bacc
    from concourse import mybir as _mybir
    from concourse.bass_utils import run_bass_kernel_spmd as _run

    x = _np.asarray(inputs["L0_attn_X"])
    n_seq, seq, d = x.shape
    rot_dim, k = d // 2, d // P
    order = _np.concatenate([_np.arange(0, rot_dim, 2), _np.arange(1, rot_dim, 2), _np.arange(rot_dim, d)])
    w_in = _np.asarray(inputs["L0_attn_W_in"])
    b_in = _np.asarray(inputs["L0_attn_b_in"])
    q_cols, k_cols, v_cols = order, order + d, order + 2 * d
    up = _np.asarray(inputs["L0_ffn_up_weight"])
    down = _np.asarray(inputs["L0_ffn_down_weight"])
    h = up.shape[0] // P

    def columns(v):
        return v.reshape(-1, P).T

    inv_freq = (_np.float32(1.0) / _np.float32(THETA) ** (_np.arange(0, rot_dim, 2, dtype=_np.float32)
                                                        / _np.float32(rot_dim))).astype(_np.float32)
    angle = (_np.arange(seq, dtype=_np.float32)[:, None] * inv_freq[None, :]).astype(_np.float32).astype(_np.float64)
    rotation = _np.stack([_np.sin(2 * angle), _np.cos(2 * angle)], axis=1).astype(_np.float32)

    arrays = {
        "x": x,
        "w_in": _np.stack([w_in[:, c].reshape(k, P, d) for c in (k_cols, v_cols, q_cols)]),
        "w_out": _np.asarray(inputs["L0_attn_W_out"])[order].reshape(k, P, d),
        "up": up.reshape(h, P, k, P).transpose(0, 3, 2, 1).reshape(h, P, k * P),
        "down": down.T.reshape(h, P, d),
        "gamma": columns(_np.asarray(inputs["L0_attn_gamma"])),
        "beta": columns(_np.asarray(inputs["L0_attn_beta"])),
        "b_kv": _np.concatenate([b_in[k_cols], b_in[v_cols]]),
        "b_q": columns(b_in[q_cols]),
        "b_out": _np.asarray(inputs["L0_attn_b_out"]),
        "up_scale": columns(_np.asarray(inputs["L0_ffn_up_scale"])),
        "down_scale": _np.asarray(inputs["L0_ffn_down_scale"]),
        "output_scale": _np.asarray(inputs["L0_ffn_output_scale"]),
        "rotation": rotation.reshape(seq // P, P, 2, rot_dim // 2).transpose(1, 0, 2, 3),
        "identity": _np.eye(P, dtype=_np.float32),
    }
    nc = _bacc.Bacc("TRN2", target_bir_lowering=False, num_devices=1)
    feeds, args = {}, []
    for name, a in arrays.items():
        feeds[f"in_{name}"] = _np.ascontiguousarray(a)
        args.append(nc.dram_tensor(f"in_{name}", a.shape, _mybir.dt.from_np(a.dtype), kind="ExternalInput").ap())
    args.append(nc.dram_tensor("out_0", x.shape, _mybir.dt.float32, kind="ExternalOutput").ap())
    attention_ffn_kernel(nc, *args)
    r = _run(nc, [feeds], core_ids=[0])
    return r.results[0]["out_0"]
```

```python
from contextlib import ExitStack

import numpy as np
import concourse.bass as bass
from concourse import mybir

P = 128
F32 = mybir.dt.float32
F32R = mybir.dt.float32r
BF16 = mybir.dt.bfloat16
ALU = mybir.AluOpType
ACT = mybir.ActivationFunctionType
EPS = 1e-5
THETA = 10000.0

SIGN_SLOTS = 4
HID_SLOTS = 4
FULL_SLOTS = 2
UP_BANKS = 3
DOWN_LAG = 2


def attention_ffn_kernel(nc, x, w_in, w_out, up, down, gamma, beta, b_kv, b_q, b_out, up_scale, down_scale,
                         output_scale, rotation, identity, out):
    NB, SEQ, D = x.shape
    R = SEQ // P
    K = D // P
    H = up.shape[0]
    HALF = D // 4
    assert SEQ == 512 and D == 512 and R == 4 and K == 4 and H > 8

    ctx = ExitStack()
    with ctx:
        def sb(name, shape, dt=F32):
            return ctx.enter_context(nc.sbuf_tensor(name, shape, dt))

        def sem(name):
            return ctx.enter_context(nc.semaphore(name))

        win_hi = sb("win_hi", [P, 3, K, D], F32R)
        win_lo = sb("win_lo", [P, 3, K, D], F32R)
        wout_hi = sb("wout_hi", [P, K, D], F32R)
        wout_lo = sb("wout_lo", [P, K, D], F32R)
        up_sign = sb("up_sign", [P, H, K, P], F32R)
        down_sign = sb("down_sign", [P, H, D], F32R)
        xz = sb("xz", [P, R, D])
        res = sb("res", [P, R, D])
        zt_hi = sb("zt_hi", [P, K, SEQ], F32R)
        zt_lo = sb("zt_lo", [P, K, SEQ], F32R)
        hid_hi = sb("hid_hi", [P, HID_SLOTS, SEQ], F32R)
        hid_lo = sb("hid_lo", [P, HID_SLOTS, SEQ], F32R)
        full = sb("full", [P, FULL_SLOTS, SEQ])
        kb = sb("kb", [P, D])
        vb = sb("vb", [P, D])
        turned = sb("turned", [P, 4, HALF])
        prod = sb("prod", [P, 6, HALF])
        acc_p = sb("acc_p", [P, 4, HALF])
        acc_r = sb("acc_r", [P, 4, HALF])
        junk = sb("junk", [P, D], BF16)
        rot = sb("rot", [P, R, 2, HALF])
        bias_kv = sb("bias_kv", [P, 2, D])
        bout_bc = sb("bout_bc", [P, D])
        dscale_bc = sb("dscale_bc", [P, D])
        ident = sb("ident", [P, P])
        gamma_c = sb("gamma_c", [P, K])
        beta_c = sb("beta_c", [P, K])
        bq_c = sb("bq_c", [P, K])
        uscale_c = sb("uscale_c", [P, H])
        oscale_c = sb("oscale_c", [P, 1])
        half_c = sb("half_c", [P, 2])
        bn = sb("bn", [P, R, 6])
        st = sb("st", [P, 8, R])
        root = sb("root", [P, 2, R])
        inv = sb("inv", [P, 2, R])
        nxt = sb("nxt", [P, 3, R])
        cur = sb("cur", [P, 3, R])
        nsq = sb("nsq", [P, R, 2])
        nrm = sb("nrm", [P, R, 2])
        nw = sb("nw", [P, 3, 2])
        wrow = sb("wrow", [P, 1])
        warm = sb("warm", [P, 1])
        v_raw = [kb[:], vb[:], acc_p[:].rearrange("p a i -> p (a i)"), acc_r[:].rearrange("p a i -> p (a i)")]
        acol = sb("acol", [P, 2, K])

        banks = [ctx.enter_context(nc.psum_tensor(f"bank{i}", [P, 512], F32)) for i in range(8)]

        gains_in = sem("gains_in")
        tables_in = sem("tables_in")
        scales_in = sem("scales_in")
        x0_in = [sem(f"x0_in{r}") for r in range(R)]
        x_in = sem("x_in")
        res_in = sem("res_in")
        piece_in = [sem(f"piece_in{i}") for i in range(K)]
        v_piece_in = [sem(f"v_piece_in{i}") for i in range(K)]
        sign_in = [sem(f"sign_in{i}") for i in range(SIGN_SLOTS)]
        out_dma = sem("out_dma")
        consts_set = sem("consts_set")
        piece_hi = sem("piece_hi")
        piece_lo = sem("piece_lo")
        v_whole = sem("v_whole")
        v_lo = sem("v_lo")
        beta_mm = sem("beta_mm")
        bias_kv_set = sem("bias_kv_set")
        betaq_mm = sem("betaq_mm")
        bq_set = sem("bq_set")
        wq_set = sem("wq_set")
        wout_set = sem("wout_set")
        pool_step = sem("pool_step")
        up_signed = sem("up_signed")
        down_signed = sem("down_signed")
        kv_mm = sem("kv_mm")
        up_mm = sem("up_mm")
        down_mm = sem("down_mm")
        a_mm = sem("a_mm")
        q_mm = sem("q_mm")
        t_mm = sem("t_mm")
        y_mm = sem("y_mm")
        squared = sem("squared")
        normed = sem("normed")
        relu_set = sem("relu_set")
        root_set = sem("root_set")
        q_set = sem("q_set")
        zt_hi_set = sem("zt_hi_set")
        kv_biased = sem("kv_biased")
        prod_set = sem("prod_set")
        crossed = sem("crossed")
        turned_set = sem("turned_set")
        summed = sem("summed")
        hid_set = sem("hid_set")
        acc_set = sem("acc_set")
        a_set = sem("a_set")
        roots_due = sem("roots_due")
        z_set = sem("z_set")
        ffn_read = sem("ffn_read")
        res_set = sem("res_set")
        q_split = sem("q_split")
        zt_set = sem("zt_set")
        out_set = sem("out_set")
        dve_step = sem("dve_step")

        block = ctx.enter_context(nc.Block())
        LAST = NB - 1

        @block.sync
        def _(sp):
            def small(dst, src, arrived):
                sp.dma_start(dst, src).then_inc(arrived, 16)

            for r in range(R):
                sp.dma_start(xz[:, r, :], x[0, r * P:(r + 1) * P, :]).then_inc(x0_in[r], 16)
                if r == 1:
                    small(gamma_c[:], gamma, gains_in)
                    small(beta_c[:], beta, gains_in)
                    small(ident[:], identity, gains_in)
            for n in range(K):
                sp.dma_start(res[:, n, :], w_in[0, n]).then_inc(piece_in[n], 16)
            for n in range(K):
                sp.dma_start(v_raw[n], w_in[1, n]).then_inc(v_piece_in[n], 16)
            small(bias_kv[:].rearrange("p a d -> p (a d)"), b_kv.partition_broadcast(P), tables_in)
            small(rot[:], rotation, tables_in)
            small(uscale_c[:], up_scale, tables_in)
            small(bq_c[:], b_q, tables_in)

            def sign_piece(n):
                if n < SIGN_SLOTS:
                    sp.wait_ge(t_mm, K)
                elif n % 2 == 0:
                    sp.wait_ge(up_signed, (n - SIGN_SLOTS) // 2 + 1)
                else:
                    sp.wait_ge(down_signed, (n - SIGN_SLOTS) // 2 + 1)
                src = (up if n % 2 == 0 else down)[n // 2]
                sp.dma_start(xz[:, n % SIGN_SLOTS, :], src).then_inc(sign_in[n % SIGN_SLOTS], 16)

            def late_piece(n):
                if n < K:
                    sp.wait_ge(piece_hi, n + 1)
                    sp.wait_ge(piece_lo, n + 1)
                    sp.wait_ge(beta_mm, n + 1)
                else:
                    sp.wait_ge(wq_set, n - K + 1)
                src = w_in[2, n] if n < K else w_out[n - K]
                sp.dma_start(res[:, n % K, :], src).then_inc(piece_in[n % K], 16)

            for n in range(K):
                late_piece(n)
            for n in range(SIGN_SLOTS):
                sign_piece(n)
            small(bout_bc[:], b_out.partition_broadcast(P), scales_in)
            small(dscale_bc[:], down_scale.partition_broadcast(P), scales_in)
            small(oscale_c[:], output_scale.partition_broadcast(P), scales_in)
            for n in range(SIGN_SLOTS, 2 * H):
                sign_piece(n)
                if 4 * K <= n < 6 * K and n % 2 == 0:
                    late_piece(K + (n - 4 * K) // 2)

            def sequence(b, first, last):
                if first:
                    sp.wait_ge(wout_set, K)
                else:
                    sp.wait_ge(out_dma, b * (16 * R))
                sp.dma_start(res[:], x[b].rearrange("(r p) d -> p r d", p=P)).then_inc(res_in, 16)
                if not last:
                    if first:
                        sp.wait_ge(up_signed, H)
                        sp.wait_ge(down_signed, H)
                    else:
                        sp.wait_ge(t_mm, b * K + K)
                    sp.dma_start(xz[:], x[b + 1].rearrange("(r p) d -> p r d", p=P)).then_inc(x_in, 16)
                for r in range(R):
                    sp.wait_ge(out_set, b * R + (r + 1))
                    sp.dma_start(out[b].rearrange("(r p) d -> r p d", p=P)[r], res[:, r, :]).then_inc(out_dma, 16)

            sequence(0, True, False)
            with sp.Fori(1, LAST) as b:
                sequence(b, False, False)
            sequence(LAST, False, True)
            sp.wait_ge(out_dma, NB * R * 16)

        @block.gpsimd
        def _(pool):
            done = [0]

            def link(ins):
                done[0] += 1
                ins.then_inc(pool_step, 1)
                pool.wait_ge(pool_step, done[0])

            def late_split(n):
                raw = res[:, n % K, :]
                hi = win_hi[:, 2, n, :] if n < K else wout_hi[:, n - K, :]
                lo = win_lo[:, 2, n, :] if n < K else wout_lo[:, n - K, :]
                pool.wait_ge(piece_in[n % K], 16 * (2 + n // K))
                if n < K:
                    pool.wait_ge(betaq_mm, n + 1)
                    link(nc.gpsimd.tensor_scalar(raw, raw, gamma_c[:, n:n + 1], None, ALU.mult))
                link(nc.gpsimd.tensor_copy(hi, raw))
                nc.gpsimd.tensor_tensor(lo, raw, hi.bitcast(F32), ALU.subtract).then_inc(wq_set if n < K else wout_set, 1)

            def turn(b, r):
                pool.wait_ge(kv_biased, b * (2 * R) + (2 * r + 2))
                if r:
                    pool.wait_ge(turned_set, b * R + r)
                nc.gpsimd.tensor_tensor(prod[:, 0, :], kb[:, 0:HALF], vb[:, HALF:2 * HALF], ALU.mult)
                nc.gpsimd.tensor_tensor(prod[:, 1, :], kb[:, HALF:2 * HALF], vb[:, 0:HALF], ALU.mult).then_inc(crossed, 1)
                pool.wait_ge(crossed, b * R + (r + 1))
                pool.wait_ge(prod_set, b * R + (r + 1))
                if r:
                    pool.wait_ge(summed, b * R + r)
                nc.gpsimd.tensor_tensor(turned[:].rearrange("p (a c) i -> p a c i", a=2),
                                        prod[:, 0:4, :].rearrange("p (a c) i -> p a c i", a=2),
                                        rot[:, r, :, :].unsqueeze(2).to_broadcast([P, 2, 2, HALF]),
                                        ALU.mult).then_inc(turned_set, 1)

            nc.gpsimd.memset(half_c[:, 0:1], 0.25).then_inc(consts_set, 1)
            nc.gpsimd.memset(half_c[:, 1:2], 0.5).then_inc(consts_set, 1)
            beta_bc = full[:, 0, :].rearrange("p (k j) -> p k j", k=K)
            link(nc.gpsimd.memset(full[:, 0, :], 1.0))
            pool.wait_ge(gains_in, 3 * 16)
            for k in range(K):
                nc.gpsimd.tensor_scalar(beta_bc[:, k, :], beta_bc[:, k, :], beta_c[:, k:k + 1], None,
                                        ALU.mult).then_inc(consts_set, 1)
            for n in range(K):
                pool.wait_ge(v_whole, n + 1)
                nc.gpsimd.tensor_tensor(win_lo[:, 1, n, :], v_raw[n], win_hi[:, 1, n, :].bitcast(F32),
                                        ALU.subtract).then_inc(v_lo, 1)
            pool.wait_ge(tables_in, 4 * 16)
            for r in range(R):
                turn(0, r)
                if r:
                    late_split(r - 1)
            for n in range(K - 1, 2 * K):
                late_split(n)
            with pool.Fori(1, NB) as b:
                for r in range(R):
                    turn(b, r)

        @block.scalar
        def _(act):
            def piece(n):
                act.wait_ge(piece_in[n], 16)
                nc.scalar.activation(win_hi[:, 0, n, :], res[:, n, :], ACT.Copy,
                                     scale=gamma_c[:, n:n + 1]).then_inc(piece_hi, 1)

            def v_piece(n):
                act.wait_ge(v_piece_in[n], 16)
                nc.scalar.activation(win_hi[:, 1, n, :], v_raw[n], ACT.Copy, scale=gamma_c[:, n:n + 1])

            def v_piece_whole(n):
                act.wait_ge(beta_mm, K + n + 1)
                nc.scalar.activation(v_raw[n], v_raw[n], ACT.Copy, scale=gamma_c[:, n:n + 1]).then_inc(v_whole, 1)

            def sign_up(c):
                n = 2 * c
                act.wait_ge(sign_in[n % SIGN_SLOTS], 16 * (n // SIGN_SLOTS + 1))
                nc.scalar.activation(up_sign[:, c].rearrange("p k h -> p (k h)"), xz[:, n % SIGN_SLOTS, :],
                                     ACT.Sign).then_inc(up_signed, 1)

            def sign_down(c):
                n = 2 * c + 1
                act.wait_ge(sign_in[n % SIGN_SLOTS], 16 * (n // SIGN_SLOTS + 1))
                nc.scalar.activation(down_sign[:, c, :], xz[:, n % SIGN_SLOTS, :], ACT.Sign).then_inc(down_signed, 1)

            def roots(b):
                act.wait_ge(roots_due, b + 1)
                nc.scalar.activation(root[:], st[:, 0:2, :], ACT.Sqrt).then_inc(root_set, 1)

            def transposed_hi(b, k):
                act.wait_ge(t_mm, b * K + (k + 1))
                nc.scalar.activation(zt_hi[:, k, :], banks[k][:], ACT.Copy).then_inc(zt_hi_set, 1)

            def norms(b, r):
                for j, src in enumerate((kb, vb)):
                    act.wait_ge(kv_biased, b * (2 * R) + (2 * r + j + 1))
                    if r + j:
                        act.wait_ge(squared, b * (2 * R) + (2 * r + j))
                    nc.scalar.activation(junk[:], src[:], ACT.Square, accum_out=nsq[:, r, j:j + 1]).then_inc(squared, 1)
                act.wait_ge(squared, b * (2 * R) + (2 * r + 2))
                nc.scalar.activation(nrm[:, r, :], nsq[:, r, :], ACT.Sqrt).then_inc(normed, 1)

            def relu(b, c):
                bank = banks[4 + c % UP_BANKS]
                act.wait_ge(up_mm, b * H + (c + 1))
                if c >= HID_SLOTS:
                    act.wait_ge(down_mm, b * H + (c - HID_SLOTS + 1))
                if c >= FULL_SLOTS:
                    act.wait_ge(hid_set, b * H + (c - FULL_SLOTS + 1))
                nc.scalar.activation(full[:, c % FULL_SLOTS, :], bank[:], ACT.Relu, scale=uscale_c[:, c:c + 1])
                nc.scalar.activation(hid_hi[:, c % HID_SLOTS, :], bank[:], ACT.Relu,
                                     scale=uscale_c[:, c:c + 1]).then_inc(relu_set, 1)

            def scaled_q(b, q):
                act.wait_ge(q_mm, b * K + (q + 1))
                if q == 0:
                    act.wait_ge(a_set, b + 1)
                    act.wait_ge(hid_set, b * H + H)
                    act.wait_ge(down_mm, b * H + H)
                if q >= FULL_SLOTS:
                    act.wait_ge(q_split, b * K + (q - FULL_SLOTS + 1))
                for dst in (full[:, q % FULL_SLOTS, :], hid_hi[:, q, :]):
                    last = nc.scalar.activation(dst, banks[4 + q][:], ACT.Identity, scale=acol[:, 0, q:q + 1],
                                                bias=acol[:, 1, q:q + 1])
                last.then_inc(q_set, 1)

            def sequence(b, first, last):
                for r in range(R):
                    norms(b, r)
                    if first:
                        if r < SIGN_SLOTS // 2:
                            sign_up(r)
                            sign_down(r)
                for c in range(H):
                    relu(b, c)
                    if first and c + SIGN_SLOTS // 2 < H:
                        sign_up(c + SIGN_SLOTS // 2)
                        sign_down(c + SIGN_SLOTS // 2)
                    if not last and not first and c == 10:
                        roots(b + 1)
                for q in range(K):
                    scaled_q(b, q)
                    if first and q == 2:
                        roots(b + 1)
                if not last:
                    for k in range(K):
                        transposed_hi(b + 1, k)

            act.wait_ge(consts_set, 2)
            nc.scalar.activation(warm[:], half_c[:, 0:1], ACT.Sqrt)
            act.wait_ge(gains_in, 3 * 16)
            for n in range(2):
                piece(n)
            roots(0)
            for n in range(2, K):
                piece(n)
            for n in range(K):
                v_piece(n)
                transposed_hi(0, n)
            for n in range(K):
                v_piece_whole(n)
            act.wait_ge(tables_in, 4 * 16)
            sequence(0, True, False)
            with act.Fori(1, LAST) as b:
                sequence(b, False, False)
            sequence(LAST, False, True)

        @block.vector
        def _(dve):
            count = [0]

            def step(ins):
                count[0] += 1
                ins.then_inc(dve_step, 1)
                return count[0]

            def landed(base, n):
                dve.wait_ge(dve_step, base + n)

            def link(base, ins):
                landed(base, step(ins))

            def newton_rsqrt(base, y, a, t):
                link(base, nc.vector.scalar_tensor_tensor(out=t, in0=y, scalar=-0.5, in1=y, op0=ALU.mult, op1=ALU.mult))
                link(base, nc.vector.tensor_tensor(t, t, a, ALU.mult))
                link(base, nc.vector.scalar_tensor_tensor(out=y, in0=t, scalar=1.5, in1=y, op0=ALU.add, op1=ALU.mult))

            def row_stats(r):
                return nc.vector.bn_stats(bn[:, r, :], xz[:, r, :])

            def moments(base):
                S = st
                step(nc.vector.tensor_tensor(S[:, 2, :], bn[:, :, 1], bn[:, :, 4], ALU.add))
                step(nc.vector.tensor_tensor(S[:, 3, :], bn[:, :, 1], bn[:, :, 4], ALU.subtract))
                link(base, nc.vector.tensor_tensor(S[:, 4, :], bn[:, :, 2], bn[:, :, 5], ALU.add))
                step(nc.vector.tensor_scalar(nxt[:, 0, :], S[:, 2, :], 0.5, None, ALU.mult))
                link(base, nc.vector.scalar_tensor_tensor(out=S[:, 5, :], in0=S[:, 3, :], scalar=0.25, in1=S[:, 3, :],
                                                          op0=ALU.mult, op1=ALU.mult))
                link(base, nc.vector.scalar_tensor_tensor(out=S[:, 6, :], in0=S[:, 4, :], scalar=1.0 / D, in1=S[:, 5, :],
                                                          op0=ALU.mult, op1=ALU.add))
                link(base, nc.vector.tensor_scalar(S[:, 0, :], S[:, 6, :], EPS, None, ALU.add))
                nc.vector.scalar_tensor_tensor(out=S[:, 1, :], in0=S[:, 0, :], scalar=EPS, in1=S[:, 6, :],
                                               op0=ALU.mult, op1=ALU.add).then_inc(roots_due, 1)

            def scales(base, b):
                dve.wait_ge(root_set, b + 1)
                link(base, nc.vector.reciprocal(inv[:], root[:]))
                newton_rsqrt(base, inv[:], st[:, 0:2, :], st[:, 2:4, :])
                step(nc.vector.tensor_scalar(nxt[:, 1, :], inv[:, 0, :], 1.0, None, ALU.add))
                link(base, nc.vector.tensor_tensor(st[:, 4, :], st[:, 1, :], inv[:, 1, :], ALU.mult))
                link(base, nc.vector.tensor_tensor(nxt[:, 2, :], st[:, 4, :], inv[:, 0, :], ALU.mult))

            def normalise(r):
                nc.vector.tensor_scalar(xz[:, r, :], xz[:, r, :], nxt[:, 0, r:r + 1], inv[:, 1, r:r + 1],
                                        ALU.subtract, ALU.mult).then_inc(z_set, 1)

            def transposed_lo(b, k):
                dve.wait_ge(zt_hi_set, b * K + (k + 1))
                nc.vector.tensor_tensor(zt_lo[:, k, :], banks[k][:], zt_hi[:, k, :].bitcast(F32),
                                        ALU.subtract).then_inc(zt_set, 1)

            def piece(n):
                dve.wait_ge(piece_hi, n + 1)
                nc.vector.scalar_tensor_tensor(out=win_lo[:, 0, n, :], in0=res[:, n, :], scalar=gamma_c[:, n:n + 1],
                                               in1=win_hi[:, 0, n, :].bitcast(F32),
                                               op0=ALU.mult, op1=ALU.subtract).then_inc(piece_lo, 1)

            def biased(base, b, r):
                landed(base, count[0])
                for j, dst in enumerate((kb, vb)):
                    dve.wait_ge(kv_mm, b * (2 * R) + (2 * r + j + 1))
                    if r:
                        dve.wait_ge(squared, b * (2 * R) + (2 * (r - 1) + j + 1))
                        dve.wait_ge(crossed, b * R + r)
                        dve.wait_ge(prod_set, b * R + r)
                    nc.vector.tensor_tensor(dst[:], banks[2 * (r % 2) + j][:], bias_kv[:, j, :],
                                            ALU.add).then_inc(kv_biased, 1)

            def products(base, b, r):
                landed(base, count[0])
                dve.wait_ge(kv_biased, b * (2 * R) + (2 * r + 2))
                if r:
                    dve.wait_ge(turned_set, b * R + r)
                nc.vector.tensor_tensor(prod[:, 2:6, :].rearrange("p a i -> p (a i)"), kb[:], vb[:],
                                        ALU.mult).then_inc(prod_set, 1)

            def accumulate(base, b, r):
                dve.wait_ge(normed, b * R + (r + 1))
                y, t = nw[:, 0, :], nw[:, 1, :]
                link(base, nc.vector.reciprocal(y, nrm[:, r, :]))
                newton_rsqrt(base, y, nsq[:, r, :], t)
                link(base, nc.vector.tensor_tensor(wrow[:], nw[:, 0, 0:1], nw[:, 0, 1:2], ALU.mult))
                flat = "p a i -> p (a i)"

                def weighted(dst, src):
                    if r == 0:
                        return nc.vector.tensor_scalar(dst, src, wrow[:, 0:1], None, ALU.mult)
                    return nc.vector.scalar_tensor_tensor(out=dst, in0=src, scalar=wrow[:, 0:1], in1=dst,
                                                          op0=ALU.mult, op1=ALU.add)

                step(weighted(acc_p[:].rearrange(flat), prod[:, 2:6, :].rearrange(flat)))
                dve.wait_ge(turned_set, b * R + (r + 1))
                if r:
                    dve.wait_ge(summed, b * R + r)
                weighted(acc_r[:].rearrange(flat), turned[:].rearrange(flat)).then_inc(summed, 1)

            def combine(base, b):
                landed(base, count[0])
                dve.wait_ge(summed, b * R + R)
                step(nc.vector.tensor_tensor(prod[:, 0, :], acc_p[:, 0, :], acc_p[:, 1, :], ALU.add))
                step(nc.vector.tensor_tensor(prod[:, 1, :], acc_r[:, 2, :], acc_r[:, 3, :], ALU.subtract))
                link(base, nc.vector.tensor_tensor(prod[:, 2, :], acc_r[:, 0, :], acc_r[:, 1, :], ALU.add))
                link(base, nc.vector.tensor_tensor(prod[:, 3, :], prod[:, 1, :], prod[:, 2, :], ALU.subtract))
                nc.vector.tensor_tensor(acc_p[:, 0, :], prod[:, 0, :], prod[:, 3, :], ALU.add)
                nc.vector.tensor_tensor(acc_p[:, 1, :], prod[:, 0, :], prod[:, 3, :], ALU.subtract).then_inc(acc_set, 1)

            def attention_scale(b):
                dve.wait_ge(a_mm, b + 1)
                nc.vector.tensor_scalar(acol[:, 0, :], banks[7][:, 0:K], 0.5, None, ALU.add).then_inc(dve_step, 1)
                count[0] += 1

            def attention_bias(base):
                landed(base, count[0])
                nc.vector.tensor_tensor(acol[:, 1, :], acol[:, 0, :], bq_c[:], ALU.mult).then_inc(a_set, 1)

            def hidden_lo(b, c):
                dve.wait_ge(relu_set, b * H + (c + 1))
                nc.vector.tensor_tensor(hid_lo[:, c % HID_SLOTS, :], full[:, c % FULL_SLOTS, :],
                                        hid_hi[:, c % HID_SLOTS, :].bitcast(F32), ALU.subtract).then_inc(hid_set, 1)

            def residual(base, b, r):
                if r == 0:
                    dve.wait_ge(res_in, b * 16 + 16)
                link(base, nc.vector.tensor_scalar(res[:, r, :], res[:, r, :], cur[:, 0, r:r + 1], cur[:, 1, r:r + 1],
                                                   ALU.subtract, ALU.mult))
                step(nc.vector.tensor_tensor(res[:, r, :], res[:, r, :], bout_bc[:], ALU.add))

            def ffn_scaled(b, r):
                dve.wait_ge(down_mm, b * H + H)
                if r >= 2:
                    dve.wait_ge(res_set, b * R + (r - 1))
                nc.vector.scalar_tensor_tensor(out=(kb, vb)[r % 2][:], in0=banks[r][:], scalar=cur[:, 2, r:r + 1],
                                               in1=dscale_bc[:], op0=ALU.mult, op1=ALU.mult).then_inc(ffn_read, 1)

            def ffn_added(b, r):
                dve.wait_ge(ffn_read, b * R + (r + 1))
                nc.vector.scalar_tensor_tensor(out=res[:, r, :], in0=(kb, vb)[r % 2][:], scalar=cur[:, 0, r:r + 1],
                                               in1=res[:, r, :], op0=ALU.add, op1=ALU.add).then_inc(res_set, 1)

            def query_lo(b, q):
                dve.wait_ge(q_set, b * K + (q + 1))
                nc.vector.tensor_tensor(hid_lo[:, q, :], full[:, q % FULL_SLOTS, :], hid_hi[:, q, :].bitcast(F32),
                                        ALU.subtract).then_inc(q_split, 1)

            def finish(b, r):
                dve.wait_ge(y_mm, b * R + (r + 1))
                dve.wait_ge(res_set, b * R + (r + 1))
                nc.vector.tensor_tensor(res[:, r, :], banks[4 + r][:], res[:, r, :], ALU.add).then_inc(out_set, 1)

            def sequence(b, first, last, base):
                count[0] = 0
                step(nc.vector.tensor_copy(cur[:], nxt[:]))
                for r in range(R):
                    biased(base, b, r)
                    if r:
                        accumulate(base, b, r - 1)
                    products(base, b, r)
                for c in range(H):
                    hidden_lo(b, c)
                    if c == 0:
                        accumulate(base, b, R - 1)
                    if c == 1:
                        combine(base, b)
                    if c == 3:
                        if first:
                            dve.wait_ge(betaq_mm, K)
                            nc.vector.tensor_tensor(bq_c[:], banks[7][:, 8:8 + K], bq_c[:], ALU.add).then_inc(bq_set, 1)
                            dve.wait_ge(bq_set, 1)
                        attention_scale(b)
                        attention_bias(base)
                    if not last and not first:
                        if 4 <= c < 4 + R:
                            if c == 4:
                                dve.wait_ge(x_in, b * 16 + 16)
                            step(row_stats(c - 4))
                        if c == 8:
                            landed(base, count[0])
                            moments(base)
                        if c == 10:
                            scales(base, b + 1)
                        if 11 <= c < 11 + R:
                            normalise(c - 11)
                    if c >= H - R and not first:
                        residual(base, b, c - (H - R))
                if first:
                    dve.wait_ge(scales_in, 3 * 16)
                    link(base, nc.vector.tensor_scalar(dscale_bc[:], dscale_bc[:], oscale_c[:, 0:1], None, ALU.mult))
                    for r in range(R):
                        residual(base, b, r)
                landed(base, count[0])
                ffn_scaled(b, 0)
                ffn_scaled(b, 1)
                ffn_added(b, 0)
                ffn_added(b, 1)
                query_lo(b, 0)
                ffn_scaled(b, 2)
                ffn_scaled(b, 3)
                ffn_added(b, 2)
                ffn_added(b, 3)
                query_lo(b, 1)
                if first:
                    dve.wait_ge(x_in, 16)
                    for r in range(R):
                        step(row_stats(r))
                    landed(base, count[0])
                    moments(base)
                query_lo(b, 2)
                if first:
                    scales(base, b + 1)
                    for r in range(R):
                        normalise(r)
                query_lo(b, 3)
                if not last:
                    for k in range(K):
                        transposed_lo(b + 1, k)
                for r in range(R):
                    finish(b, r)
                return count[0]

            for r in range(R):
                dve.wait_ge(x0_in[r], 16)
                step(row_stats(r))
            landed(0, count[0])
            moments(0)
            for n in range(2):
                piece(n)
            scales(0, 0)
            for r in range(R):
                normalise(r)
            for n in range(2, K):
                piece(n)
            for k in range(K):
                transposed_lo(0, k)
            dve.wait_ge(tables_in, 4 * 16)
            for j in range(2):
                dve.wait_ge(beta_mm, K * (j + 1))
                nc.vector.tensor_tensor(bias_kv[:, j, :], banks[4 + j][:], bias_kv[:, j, :], ALU.add).then_inc(bias_kv_set, 1)
            dve.wait_ge(bias_kv_set, 2)
            dve.wait_ge(v_lo, K)
            start = count[0]
            n0 = sequence(0, True, False, start)
            per = n0 - 1
            with dve.Fori(1, LAST) as b:
                assert sequence(b, False, False, b * per + (start + 1)) == per
            sequence(LAST, False, True, LAST * per + (start + 1))

        @block.tensor
        def _(pe):
            mm = nc.tensor.matmul

            def three_pass(dst, l_hi, l_lo, r_hi, r_lo, k):
                mm(dst, l_hi, r_hi, start=(k == 0), stop=False)
                mm(dst, l_lo, r_hi, start=False, stop=False)
                return mm(dst, l_hi, r_lo, start=False, stop=(k == K - 1))

            def transposes(b, k):
                for r in range(R):
                    last = nc.tensor.transpose(banks[k][:, r * P:(r + 1) * P], xz[:, r, k * P:(k + 1) * P], ident[:])
                last.then_inc(t_mm, 1)

            def keys_values(b, r, first):
                for j in range(2):
                    bank = banks[2 * (r % 2) + j]
                    if r >= 2:
                        pe.wait_ge(kv_biased, b * (2 * R) + (2 * (r - 2) + j + 1))
                    for k in range(K):
                        s = slice(r * P, (r + 1) * P)
                        if r == 0 and j == 0:
                            pe.wait_ge(zt_set, b * K + (k + 1))
                        if first and r == 0:
                            if j == 0:
                                pe.wait_ge(piece_lo, k + 1)
                            else:
                                pe.wait_ge(v_lo, k + 1)
                        last = three_pass(bank[:], zt_hi[:, k, s], zt_lo[:, k, s], win_hi[:, j, k, :],
                                          win_lo[:, j, k, :], k)
                    last.then_inc(kv_mm, 1)

            def up_proj(b, c, first):
                bank = banks[4 + c % UP_BANKS]
                if c >= UP_BANKS:
                    pe.wait_ge(relu_set, b * H + (c - UP_BANKS + 1))
                if first:
                    pe.wait_ge(up_signed, c + 1)
                for k in range(K):
                    mm(bank[:], up_sign[:, c, k, :], zt_hi[:, k, :], start=(k == 0), stop=False)
                    last = mm(bank[:], up_sign[:, c, k, :], zt_lo[:, k, :], start=False, stop=(k == K - 1))
                last.then_inc(up_mm, 1)

            def down_proj(b, c, first):
                pe.wait_ge(hid_set, b * H + (c + 1))
                if first:
                    pe.wait_ge(down_signed, c + 1)
                for r in range(R):
                    s = slice(r * P, (r + 1) * P)
                    mm(banks[r][:], hid_hi[:, c % HID_SLOTS, s], down_sign[:, c, :], start=(c == 0), stop=False)
                    last = mm(banks[r][:], hid_lo[:, c % HID_SLOTS, s], down_sign[:, c, :], start=False,
                              stop=(c == H - 1))
                last.then_inc(down_mm, 1)

            def beta_query(n):
                pe.wait_ge(piece_in[n], 2 * 16)
                for q in range(K):
                    last = mm(banks[7][:, 8 + q:9 + q], res[:, n, q * P:(q + 1) * P], beta_c[:, n:n + 1],
                              start=(n == 0 and q == 0), stop=(n == K - 1), skip_group_check=True)
                last.then_inc(betaq_mm, 1)

            def row_sums(b):
                pe.wait_ge(acc_set, b + 1)
                for q in range(K):
                    last = mm(banks[7][:, q:q + 1], acc_p[:, q, :], half_c[:, q // 2:q // 2 + 1], start=True, stop=True)
                last.then_inc(a_mm, 1)

            def sequence(b, first, last):
                for r in range(R):
                    if r == 1:
                        pe.wait_ge(zt_set, b * K + K)
                    keys_values(b, r, first)
                    if first and r == 1:
                        for n in range(K):
                            beta_query(n)
                if first:
                    pe.wait_ge(bias_kv_set, 2)
                else:
                    pe.wait_ge(out_set, b * R)
                for c in range(H + DOWN_LAG):
                    if c < H:
                        up_proj(b, c, first)
                    if c == DOWN_LAG:
                        pe.wait_ge(kv_biased, b * (2 * R) + 2 * R)
                    if c >= DOWN_LAG:
                        down_proj(b, c - DOWN_LAG, first)
                    if c == 4:
                        if first:
                            pe.wait_ge(bq_set, 1)
                        row_sums(b)
                pe.wait_ge(relu_set, b * H + H)
                pe.wait_ge(a_set, b + 1)
                if first:
                    pe.wait_ge(wq_set, K)
                for q in range(K):
                    s = slice(q * P, (q + 1) * P)
                    for k in range(K):
                        done = three_pass(banks[4 + q][:], win_hi[:, 2, k, s], win_lo[:, 2, k, s], zt_hi[:, k, :],
                                          zt_lo[:, k, :], k)
                    done.then_inc(q_mm, 1)
                if not last:
                    pe.wait_ge(z_set, b * R + 2 * R)
                    for k in range(K):
                        pe.wait_ge(ffn_read, b * R + (k + 1))
                        transposes(b + 1, k)
                if first:
                    pe.wait_ge(wout_set, K)
                for r in range(R):
                    s = slice(r * P, (r + 1) * P)
                    for k in range(K):
                        if r == 0:
                            pe.wait_ge(q_split, b * K + (k + 1))
                        done = three_pass(banks[4 + r][:], hid_hi[:, k, s], hid_lo[:, k, s], wout_hi[:, k, :],
                                          wout_lo[:, k, :], k)
                    done.then_inc(y_mm, 1)

            beta_bc = full[:, 0, :].rearrange("p (k j) -> p k j", k=K)

            def beta_kv(n):
                piece, raw = (piece_in[n], res[:, n, :]) if n < K else (v_piece_in[n - K], v_raw[n - K])
                pe.wait_ge(piece, 16)
                pe.wait_ge(consts_set, 3 + n % K)
                mm(banks[4 + n // K][:], beta_bc[:, n % K, :], raw, start=(n % K == 0),
                   stop=(n % K == K - 1)).then_inc(beta_mm, 1)

            for n in range(K):
                beta_kv(n)
            pe.wait_ge(gains_in, 3 * 16)
            for r in range(R):
                pe.wait_ge(z_set, r + 1)
                for k in range(K):
                    last = nc.tensor.transpose(banks[k][:, r * P:(r + 1) * P], xz[:, r, k * P:(k + 1) * P], ident[:])
                    if r == R - 1:
                        last.then_inc(t_mm, 1)
            for n in range(K, 2 * K):
                beta_kv(n)
            sequence(0, True, False)
            with pe.Fori(1, LAST) as b:
                sequence(b, False, False)
            sequence(LAST, False, True)


def kernel(**inputs):
    import numpy as _np
    import concourse.bacc as _bacc
    from concourse import mybir as _mybir
    from concourse.bass_utils import run_bass_kernel_spmd as _run

    x = _np.asarray(inputs["L0_attn_X"])
    n_seq, seq, d = x.shape
    rot_dim, k = d // 2, d // P
    order = _np.concatenate([_np.arange(0, rot_dim, 2), _np.arange(1, rot_dim, 2), _np.arange(rot_dim, d)])
    w_in = _np.asarray(inputs["L0_attn_W_in"])
    b_in = _np.asarray(inputs["L0_attn_b_in"])
    q_cols, k_cols, v_cols = order, order + d, order + 2 * d
    up = _np.asarray(inputs["L0_ffn_up_weight"])
    down = _np.asarray(inputs["L0_ffn_down_weight"])
    h = up.shape[0] // P

    def columns(v):
        return v.reshape(-1, P).T

    inv_freq = (_np.float32(1.0) / _np.float32(THETA) ** (_np.arange(0, rot_dim, 2, dtype=_np.float32)
                                                        / _np.float32(rot_dim))).astype(_np.float32)
    angle = (_np.arange(seq, dtype=_np.float32)[:, None] * inv_freq[None, :]).astype(_np.float32).astype(_np.float64)
    rotation = _np.stack([_np.sin(2 * angle), _np.cos(2 * angle)], axis=1).astype(_np.float32)

    arrays = {
        "x": x,
        "w_in": _np.stack([w_in[:, c].reshape(k, P, d) for c in (k_cols, v_cols, q_cols)]),
        "w_out": _np.asarray(inputs["L0_attn_W_out"])[order].reshape(k, P, d),
        "up": up.reshape(h, P, k, P).transpose(0, 3, 2, 1).reshape(h, P, k * P),
        "down": down.T.reshape(h, P, d),
        "gamma": columns(_np.asarray(inputs["L0_attn_gamma"])),
        "beta": columns(_np.asarray(inputs["L0_attn_beta"])),
        "b_kv": _np.concatenate([b_in[k_cols], b_in[v_cols]]),
        "b_q": columns(b_in[q_cols]),
        "b_out": _np.asarray(inputs["L0_attn_b_out"]),
        "up_scale": columns(_np.asarray(inputs["L0_ffn_up_scale"])),
        "down_scale": _np.asarray(inputs["L0_ffn_down_scale"]),
        "output_scale": _np.asarray(inputs["L0_ffn_output_scale"]),
        "rotation": rotation.reshape(seq // P, P, 2, rot_dim // 2).transpose(1, 0, 2, 3),
        "identity": _np.eye(P, dtype=_np.float32),
    }
    nc = _bacc.Bacc("TRN2", target_bir_lowering=False, num_devices=1)
    feeds, args = {}, []
    for name, a in arrays.items():
        feeds[f"in_{name}"] = _np.ascontiguousarray(a)
        args.append(nc.dram_tensor(f"in_{name}", a.shape, _mybir.dt.from_np(a.dtype), kind="ExternalInput").ap())
    args.append(nc.dram_tensor("out_0", x.shape, _mybir.dt.float32, kind="ExternalOutput").ap())
    attention_ffn_kernel(nc, *args)
    r = _run(nc, [feeds], core_ids=[0])
    return r.results[0]["out_0"]
```

```python
from contextlib import ExitStack

import numpy as np
import concourse.bass as bass
from concourse import mybir

P = 128
F32 = mybir.dt.float32
F32R = mybir.dt.float32r
BF16 = mybir.dt.bfloat16
ALU = mybir.AluOpType
ACT = mybir.ActivationFunctionType
EPS = 1e-5
THETA = 10000.0

SIGN_SLOTS = 4
HID_SLOTS = 4
FULL_SLOTS = 2
AHEAD = 6
UP_BANKS = 3
DOWN_LAG = 2


def attention_ffn_kernel(nc, x, x_cols, w_in, w_out, up, down, gamma, beta, b_kv, b_q, b_out, up_scale, down_scale,
                         output_scale, rotation, identity, row_scales, out):
    NB, SEQ, D = x.shape
    R = SEQ // P
    K = D // P
    H = up.shape[0]
    HALF = D // 4
    assert SEQ == 512 and D == 512 and R == 4 and K == 4 and H > 8

    ctx = ExitStack()
    with ctx:
        def sb(name, shape, dt=F32):
            return ctx.enter_context(nc.sbuf_tensor(name, shape, dt))

        def sem(name):
            return ctx.enter_context(nc.semaphore(name))

        win_hi = sb("win_hi", [P, 3, K, D], F32R)
        win_lo = sb("win_lo", [P, 3, K, D], F32R)
        wout_hi = sb("wout_hi", [P, K, D], F32R)
        wout_lo = sb("wout_lo", [P, K, D], F32R)
        up_sign = sb("up_sign", [P, H, K, P], F32R)
        down_sign = sb("down_sign", [P, H, D], F32R)
        xz = sb("xz", [P, R, D])
        res = sb("res", [P, R, D])
        zt_hi = sb("zt_hi", [P, K, SEQ], F32R)
        zt_lo = sb("zt_lo", [P, K, SEQ], F32R)
        hid_hi = sb("hid_hi", [P, HID_SLOTS, SEQ], F32R)
        hid_lo = sb("hid_lo", [P, HID_SLOTS, SEQ], F32R)
        full = sb("full", [P, FULL_SLOTS, SEQ])
        kvb = sb("kvb", [P, 2, D])
        kb, vb = kvb[:, 0, :], kvb[:, 1, :]
        turned = sb("turned", [P, 4, HALF])
        prod = sb("prod", [P, 6, HALF])
        acc_p = sb("acc_p", [P, 4, HALF])
        acc_r = sb("acc_r", [P, 4, HALF])
        junk = sb("junk", [P, D], BF16)
        rot = sb("rot", [P, R, 2, HALF])
        bias_kv = sb("bias_kv", [P, 2, D])
        bout_bc = sb("bout_bc", [P, D])
        dscale_bc = sb("dscale_bc", [P, D])
        ident = sb("ident", [P, P])
        gamma_c = sb("gamma_c", [P, K])
        beta_c = sb("beta_c", [P, K])
        bq_c = sb("bq_c", [P, K])
        uscale_c = sb("uscale_c", [P, H])
        oscale_c = sb("oscale_c", [P, 1])
        half_c = sb("half_c", [P, 3])
        bn = sb("bn", [P, R, 6])
        st = sb("st", [P, 8, R])
        root = sb("root", [P, 2, R])
        inv = sb("inv", [P, 2, R])
        nxt = sb("nxt", [P, 4, R])
        cur = sb("cur", [P, 3, R])
        nsq = sb("nsq", [P, R, 2])
        nrm = sb("nrm", [P, R, 2])
        nw = sb("nw", [P, 3, 2])
        wrow = sb("wrow", [P, 1])
        warm = sb("warm", [P, 1])
        x_rows = [kb, vb, turned[:].rearrange("p a i -> p (a i)"), acc_r[:].rearrange("p a i -> p (a i)")]
        v_raw = [kb, vb, acc_p[:].rearrange("p a i -> p (a i)"), acc_r[:].rearrange("p a i -> p (a i)")]
        beta_prod = dscale_bc[:]
        beta_sum = [full[:, 1, :], bout_bc[:]]
        beta_bc = full[:, 0, :].rearrange("p (k j) -> p k j", k=K)
        ones = prod[:, 5, :]
        acol = sb("acol", [P, 2, K])

        banks = [ctx.enter_context(nc.psum_tensor(f"bank{i}", [P, 512], F32)) for i in range(8)]

        gains_in = sem("gains_in")
        tables_in = sem("tables_in")
        scales_in = sem("scales_in")
        x0_in = [sem(f"x0_in{r}") for r in range(R)]
        x_in = sem("x_in")
        x_rows_in = sem("x_rows_in")
        scales_out = sem("scales_out")
        row_scales_in = sem("row_scales_in")
        res_in = sem("res_in")
        piece_in = [sem(f"piece_in{i}") for i in range(K)]
        v_piece_in = [sem(f"v_piece_in{i}") for i in range(K)]
        sign_in = [sem(f"sign_in{i}") for i in range(SIGN_SLOTS)]
        out_dma = sem("out_dma")
        consts_set = sem("consts_set")
        piece_hi = sem("piece_hi")
        piece_lo = sem("piece_lo")
        beta_mm = sem("beta_mm")
        beta_summed = sem("beta_summed")
        beta_v_mm = sem("beta_v_mm")
        bias_kv_set = sem("bias_kv_set")
        bias_q_mm = sem("bias_q_mm")
        bq_set = sem("bq_set")
        wq_set = sem("wq_set")
        wout_set = sem("wout_set")
        pool_step = sem("pool_step")
        split_step = sem("split_step")
        up_signed = sem("up_signed")
        down_signed = sem("down_signed")
        kv_mm = sem("kv_mm")
        up_mm = sem("up_mm")
        down_mm = sem("down_mm")
        a_mm = sem("a_mm")
        q_mm = sem("q_mm")
        t_mm = sem("t_mm")
        y_mm = sem("y_mm")
        squared = sem("squared")
        normed = sem("normed")
        relu_set = sem("relu_set")
        root_set = sem("root_set")
        q_set = sem("q_set")
        zt_hi_set = sem("zt_hi_set")
        kv_biased = sem("kv_biased")
        prod_set = sem("prod_set")
        crossed = sem("crossed")
        turned_set = sem("turned_set")
        summed = sem("summed")
        hid_set = sem("hid_set")
        acc_set = sem("acc_set")
        a_set = sem("a_set")
        stats_set = sem("stats_set")
        roots_due = sem("roots_due")
        z_set = sem("z_set")
        ffn_read = sem("ffn_read")
        res_set = sem("res_set")
        q_split = sem("q_split")
        zt_set = sem("zt_set")
        out_set = sem("out_set")
        dve_step = sem("dve_step")

        block = ctx.enter_context(nc.Block())
        LAST = NB - 1

        @block.sync
        def _(sp):
            def small(dst, src, arrived):
                sp.dma_start(dst, src).then_inc(arrived, 16)

            def first_rows(r):
                sp.dma_start(xz[:, r, :], x[0, r * P:(r + 1) * P, :]).then_inc(x0_in[r], 16)

            first_rows(0)
            first_rows(1)
            small(gamma_c[:], gamma, gains_in)
            small(beta_c[:], beta, gains_in)
            small(ident[:], identity, gains_in)
            for n in range(K):
                sp.dma_start(res[:, n, :], w_in[0, n]).then_inc(piece_in[n], 16)
            for n in range(K):
                sp.dma_start(v_raw[n], w_in[1, n]).then_inc(v_piece_in[n], 16)
            first_rows(2)
            first_rows(3)
            small(bias_kv[:].rearrange("p a d -> p (a d)"), b_kv.partition_broadcast(P), tables_in)
            small(rot[:], rotation, tables_in)
            small(uscale_c[:], up_scale, tables_in)
            small(bq_c[:], b_q, tables_in)

            def sign_piece(n):
                if n < SIGN_SLOTS:
                    sp.wait_ge(t_mm, n + 1)
                elif n % 2 == 0:
                    sp.wait_ge(up_signed, (n - SIGN_SLOTS) // 2 + 1)
                else:
                    sp.wait_ge(down_signed, (n - SIGN_SLOTS) // 2 + 1)
                src = (up if n % 2 == 0 else down)[n // 2]
                sp.dma_start(xz[:, n % SIGN_SLOTS, :], src).then_inc(sign_in[n % SIGN_SLOTS], 16)

            def late_piece(n):
                if n < K:
                    sp.wait_ge(piece_hi, n + 1)
                    sp.wait_ge(piece_lo, n + 1)
                    sp.wait_ge(beta_mm, n + 1)
                else:
                    sp.wait_ge(wq_set, n - K + 1)
                src = w_in[2, n] if n < K else w_out[n - K]
                sp.dma_start(res[:, n % K, :], src).then_inc(piece_in[n % K], 16)

            def load_rows(b):
                sp.wait_ge(acc_set, b + 1)
                for t in range(R):
                    sp.dma_start(x_rows[t], x[b + 1].rearrange("(r p) d -> r p d", p=P)[t]).then_inc(x_rows_in, 16)

            for n in range(K):
                late_piece(n)
            for n in range(SIGN_SLOTS):
                sign_piece(n)
            for n in range(SIGN_SLOTS, 2 * H):
                sign_piece(n)
                if 4 * K <= n < 6 * K and n % 2 == 0:
                    late_piece(K + (n - 4 * K) // 2)
                if n == 5 * K:
                    load_rows(0)

            def sequence(b, first, last):
                def load_cols():
                    sp.dma_start(xz[:], x_cols[b + 1].rearrange("k p s -> p k s")).then_inc(x_in, 16)

                def store_scales():
                    sp.wait_ge(stats_set, b + 1)
                    sp.dma_start(row_scales[b + 1], nxt[:, 0:2, :]).then_inc(scales_out, 16)

                def spread_scales():
                    sp.wait_ge(scales_out, b * 16 + 16)
                    sp.dma_start(kvb[:].rearrange("p a d -> p (a d)"),
                                 row_scales[b + 1].rearrange("p a r -> (p a r)").partition_broadcast(P)
                                 ).then_inc(row_scales_in, 16)

                if first:
                    store_scales()
                    sp.wait_ge(up_signed, H)
                    sp.wait_ge(down_signed, H)
                    load_cols()
                    spread_scales()
                    sp.wait_ge(bias_q_mm, 1)
                    small(bout_bc[:], b_out.partition_broadcast(P), scales_in)
                    small(dscale_bc[:], down_scale.partition_broadcast(P), scales_in)
                    small(oscale_c[:], output_scale.partition_broadcast(P), scales_in)
                    sp.wait_ge(wout_set, K)
                elif not last:
                    sp.wait_ge(zt_set, b * K + K)
                    load_cols()
                if not first:
                    sp.wait_ge(out_dma, b * (16 * R))
                sp.dma_start(res[:], x[b].rearrange("(r p) d -> p r d", p=P)).then_inc(res_in, 16)
                if not first and not last:
                    load_rows(b)
                    store_scales()
                    spread_scales()
                for r in range(R):
                    sp.wait_ge(out_set, b * R + (r + 1))
                    sp.dma_start(out[b].rearrange("(r p) d -> r p d", p=P)[r], res[:, r, :]).then_inc(out_dma, 16)

            sequence(0, True, False)
            with sp.Fori(1, LAST) as b:
                sequence(b, False, False)
            sequence(LAST, False, True)
            sp.wait_ge(out_dma, NB * R * 16)

        @block.gpsimd
        def _(pool):
            done = [0]

            def link(ins):
                done[0] += 1
                ins.then_inc(pool_step, 1)
                pool.wait_ge(pool_step, done[0])

            def late_split(n):
                raw = res[:, n % K, :]
                hi = win_hi[:, 2, n, :] if n < K else wout_hi[:, n - K, :]
                lo = win_lo[:, 2, n, :] if n < K else wout_lo[:, n - K, :]
                gain = gamma_c[:, n:n + 1] if n < K else 1.0
                pool.wait_ge(piece_in[n % K], 16 * (2 + n // K))
                nc.gpsimd.tensor_scalar(hi, raw, gain, 1.0, ALU.mult, ALU.mult).then_inc(split_step, 1)
                if n < K:
                    pool.wait_ge(beta_summed, K + (n + 1))
                    pool.wait_ge(split_step, n + 1)
                    link(nc.gpsimd.tensor_scalar(raw, raw, gain, 1.0, ALU.mult, ALU.mult))
                pool.wait_ge(split_step, n + 1)
                nc.gpsimd.tensor_tensor(lo, raw, hi.bitcast(F32), ALU.subtract).then_inc(wq_set if n < K else wout_set, 1)

            def sum_beta(part, n):
                arrived, raw = (v_piece_in[n], v_raw[n]) if part == 0 else (piece_in[n], res[:, n, :])
                pool.wait_ge(arrived, 16 * (part + 1))
                if n == 0:
                    nc.gpsimd.tensor_scalar(beta_sum[part], raw, beta_c[:, 0:1], 1.0, ALU.mult,
                                            ALU.mult).then_inc(beta_summed, 1)
                else:
                    pool.wait_ge(beta_summed, part * K + n)
                    link(nc.gpsimd.tensor_scalar(beta_prod, raw, beta_c[:, n:n + 1], 1.0, ALU.mult, ALU.mult))
                    nc.gpsimd.tensor_tensor(beta_sum[part], beta_sum[part], beta_prod, ALU.add).then_inc(beta_summed, 1)

            def turn(b, r):
                pool.wait_ge(kv_biased, b * (2 * R) + (2 * r + 2))
                if r:
                    pool.wait_ge(turned_set, b * R + r)
                nc.gpsimd.tensor_tensor(prod[:, 0, :], kb[:, 0:HALF], vb[:, HALF:2 * HALF], ALU.mult)
                nc.gpsimd.tensor_tensor(prod[:, 1, :], kb[:, HALF:2 * HALF], vb[:, 0:HALF], ALU.mult).then_inc(crossed, 1)
                pool.wait_ge(crossed, b * R + (r + 1))
                pool.wait_ge(prod_set, b * R + (r + 1))
                if r:
                    pool.wait_ge(summed, b * R + r)
                nc.gpsimd.tensor_tensor(turned[:].rearrange("p (a c) i -> p a c i", a=2),
                                        prod[:, 0:4, :].rearrange("p (a c) i -> p a c i", a=2),
                                        rot[:, r, :, :].unsqueeze(2).to_broadcast([P, 2, 2, HALF]),
                                        ALU.mult).then_inc(turned_set, 1)

            nc.gpsimd.memset(half_c[:, 0:1], 0.25).then_inc(consts_set, 1)
            nc.gpsimd.memset(half_c[:, 1:2], 0.5).then_inc(consts_set, 1)
            nc.gpsimd.memset(half_c[:, 2:3], 1.0).then_inc(consts_set, 1)
            nc.gpsimd.memset(ones, 1.0).then_inc(consts_set, 1)
            pool.wait_ge(gains_in, 3 * 16)
            pool.wait_ge(consts_set, 4)
            for k in range(K):
                nc.gpsimd.tensor_scalar(beta_bc[:, k, :], ones, beta_c[:, k:k + 1], 1.0, ALU.mult,
                                        ALU.mult).then_inc(consts_set, 1)
            for n in range(K):
                sum_beta(0, n)
            pool.wait_ge(tables_in, 4 * 16)
            for r in range(R):
                turn(0, r)
                sum_beta(1, r)
            for n in range(2 * K):
                late_split(n)
            with pool.Fori(1, NB) as b:
                for r in range(R):
                    turn(b, r)

        @block.scalar
        def _(act):
            def piece(n):
                arrived, raw = (piece_in[n], res[:, n, :]) if n < K else (v_piece_in[n - K], v_raw[n - K])
                act.wait_ge(arrived, 16)
                nc.scalar.activation(win_hi[:, n // K, n % K, :], raw, ACT.Copy,
                                     scale=gamma_c[:, n % K:n % K + 1]).then_inc(piece_hi, 1)

            def sign_up(c):
                n = 2 * c
                act.wait_ge(sign_in[n % SIGN_SLOTS], 16 * (n // SIGN_SLOTS + 1))
                nc.scalar.activation(up_sign[:, c].rearrange("p k h -> p (k h)"), xz[:, n % SIGN_SLOTS, :],
                                     ACT.Sign).then_inc(up_signed, 1)

            def sign_down(c):
                n = 2 * c + 1
                act.wait_ge(sign_in[n % SIGN_SLOTS], 16 * (n // SIGN_SLOTS + 1))
                nc.scalar.activation(down_sign[:, c, :], xz[:, n % SIGN_SLOTS, :], ACT.Sign).then_inc(down_signed, 1)

            def roots(n, rows):
                act.wait_ge(roots_due, n)
                nc.scalar.activation(root[:, :, rows], st[:, 0:2, rows], ACT.Sqrt).then_inc(root_set, 1)

            def transposed_hi(r, bank):
                act.wait_ge(t_mm, r + 1)
                nc.scalar.activation(zt_hi[:, :, r * P:(r + 1) * P], bank[:].rearrange("p (k s) -> p k s", k=K),
                                     ACT.Copy).then_inc(zt_hi_set, 1)

            def split_hi(b, k):
                act.wait_ge(z_set, b * K + (k + 1))
                act.wait_ge(q_mm, b * K)
                nc.scalar.activation(zt_hi[:, k, :], xz[:, k, :], ACT.Copy).then_inc(zt_hi_set, 1)

            def norms(b, r):
                for j, src in enumerate((kb, vb)):
                    act.wait_ge(kv_biased, b * (2 * R) + (2 * r + j + 1))
                    if r + j:
                        act.wait_ge(squared, b * (2 * R) + (2 * r + j))
                    nc.scalar.activation(junk[:], src[:], ACT.Square, accum_out=nsq[:, r, j:j + 1]).then_inc(squared, 1)
                act.wait_ge(squared, b * (2 * R) + (2 * r + 2))
                nc.scalar.activation(nrm[:, r, :], nsq[:, r, :], ACT.Sqrt).then_inc(normed, 1)

            def relu(b, c):
                bank = banks[4 + c % UP_BANKS]
                act.wait_ge(up_mm, b * H + (c + 1))
                if c >= HID_SLOTS:
                    act.wait_ge(down_mm, b * H + (c - HID_SLOTS + 1))
                if c >= FULL_SLOTS:
                    act.wait_ge(hid_set, b * H + (c - FULL_SLOTS + 1))
                nc.scalar.activation(full[:, c % FULL_SLOTS, :], bank[:], ACT.Relu, scale=uscale_c[:, c:c + 1])
                nc.scalar.activation(hid_hi[:, c % HID_SLOTS, :], bank[:], ACT.Relu,
                                     scale=uscale_c[:, c:c + 1]).then_inc(relu_set, 1)

            def scaled_q(b, q):
                act.wait_ge(q_mm, b * K + (q + 1))
                if q == 0:
                    act.wait_ge(a_set, b + 1)
                    act.wait_ge(hid_set, b * H + H)
                    act.wait_ge(down_mm, b * H + H)
                if q >= FULL_SLOTS:
                    act.wait_ge(q_split, b * K + (q - FULL_SLOTS + 1))
                for dst in (full[:, q % FULL_SLOTS, :], hid_hi[:, q, :]):
                    last = nc.scalar.activation(dst, banks[4 + q][:], ACT.Identity, scale=acol[:, 0, q:q + 1],
                                                bias=acol[:, 1, q:q + 1])
                last.then_inc(q_set, 1)

            def sequence(b, first, last):
                for r in range(R):
                    if first and r == 0:
                        transposed_hi(2, banks[4])
                        transposed_hi(3, banks[5])
                    norms(b, r)
                    if first:
                        for c in range(2 * r, min(2 * r + 2, AHEAD)):
                            sign_up(c)
                            sign_down(c)
                for c in range(H):
                    relu(b, c)
                    if first and c + AHEAD < H:
                        sign_up(c + AHEAD)
                        sign_down(c + AHEAD)
                    if not last and c == 9:
                        roots(b + 3, slice(0, R))
                for q in range(K):
                    scaled_q(b, q)
                if not last:
                    for k in range(K):
                        split_hi(b + 1, k)

            act.wait_ge(consts_set, 2)
            nc.scalar.activation(warm[:], half_c[:, 0:1], ACT.Sqrt)
            act.wait_ge(gains_in, 3 * 16)
            piece(0)
            piece(1)
            roots(1, slice(0, 2))
            piece(2)
            piece(3)
            transposed_hi(0, banks[4])
            transposed_hi(1, banks[5])
            for n in range(K, 2 * K):
                piece(n)
            roots(2, slice(2, R))
            act.wait_ge(tables_in, 4 * 16)
            sequence(0, True, False)
            with act.Fori(1, LAST) as b:
                sequence(b, False, False)
            sequence(LAST, False, True)

        @block.vector
        def _(dve):
            count = [0]

            def step(ins):
                count[0] += 1
                ins.then_inc(dve_step, 1)
                return count[0]

            def landed(base, n):
                dve.wait_ge(dve_step, base + n)

            def link(base, ins):
                landed(base, step(ins))

            def newton_rsqrt(base, y, a, t):
                link(base, nc.vector.scalar_tensor_tensor(out=t, in0=y, scalar=-0.5, in1=y, op0=ALU.mult, op1=ALU.mult))
                link(base, nc.vector.tensor_tensor(t, t, a, ALU.mult))
                link(base, nc.vector.scalar_tensor_tensor(out=y, in0=t, scalar=1.5, in1=y, op0=ALU.add, op1=ALU.mult))

            def row_stats(r, rows):
                return nc.vector.bn_stats(bn[:, r, :], rows)

            def moments(base, rows):
                def S(n):
                    return st[:, n, rows]

                def B(n):
                    return bn[:, rows, n]

                step(nc.vector.tensor_tensor(S(2), B(1), B(4), ALU.add))
                step(nc.vector.tensor_tensor(S(3), B(1), B(4), ALU.subtract))
                link(base, nc.vector.tensor_tensor(S(4), B(2), B(5), ALU.add))
                step(nc.vector.tensor_scalar(nxt[:, 1, rows], S(2), 0.5, None, ALU.mult))
                link(base, nc.vector.scalar_tensor_tensor(out=S(5), in0=S(3), scalar=0.25, in1=S(3),
                                                          op0=ALU.mult, op1=ALU.mult))
                link(base, nc.vector.scalar_tensor_tensor(out=S(6), in0=S(4), scalar=1.0 / D, in1=S(5),
                                                          op0=ALU.mult, op1=ALU.add))
                link(base, nc.vector.tensor_scalar(S(0), S(6), EPS, None, ALU.add))
                nc.vector.scalar_tensor_tensor(out=S(1), in0=S(0), scalar=EPS, in1=S(6),
                                               op0=ALU.mult, op1=ALU.add).then_inc(roots_due, 1)

            def scales(base, n, rows):
                dve.wait_ge(root_set, n)
                link(base, nc.vector.reciprocal(inv[:, :, rows], root[:, :, rows]))
                newton_rsqrt(base, inv[:, :, rows], st[:, 0:2, rows], st[:, 2:4, rows])
                step(nc.vector.tensor_scalar(nxt[:, 2, rows], inv[:, 0, rows], 1.0, None, ALU.add))
                link(base, nc.vector.tensor_tensor(st[:, 4, rows], st[:, 1, rows], inv[:, 1, rows], ALU.mult))
                step(nc.vector.tensor_tensor(nxt[:, 3, rows], st[:, 4, rows], inv[:, 0, rows], ALU.mult))

            def normalise(r):
                nc.vector.tensor_scalar(xz[:, r, :], xz[:, r, :], nxt[:, 1, r:r + 1], inv[:, 1, r:r + 1],
                                        ALU.subtract, ALU.mult).then_inc(z_set, 1)

            def normalise_cols(base, b, k):
                scale, mean = (kvb[:].rearrange("p a (q e) -> p (a q) e", e=2 * R)[:, :, a * R:(a + 1) * R]
                               .rearrange("p q r -> p r q") for a in range(2))
                chunk = xz[:, k, :].rearrange("p (r q) -> p r q", r=R)
                if k == 0:
                    dve.wait_ge(x_in, b * 16 + 16)
                    dve.wait_ge(row_scales_in, b * 16 + 16)
                link(base, nc.vector.tensor_tensor(chunk, chunk, mean, ALU.subtract))
                nc.vector.tensor_tensor(chunk, chunk, scale, ALU.mult).then_inc(z_set, 1)

            def split_lo(b, k):
                dve.wait_ge(zt_hi_set, b * K + (k + 1))
                nc.vector.tensor_tensor(zt_lo[:, k, :], xz[:, k, :], zt_hi[:, k, :].bitcast(F32),
                                        ALU.subtract).then_inc(zt_set, 1)

            def transposed_lo(r, bank):
                dve.wait_ge(zt_hi_set, r + 1)
                s = slice(r * P, (r + 1) * P)
                nc.vector.tensor_tensor(zt_lo[:, :, s], bank[:].rearrange("p (k s) -> p k s", k=K),
                                        zt_hi[:, :, s].bitcast(F32), ALU.subtract).then_inc(zt_set, 1)

            def piece(n):
                dve.wait_ge(piece_hi, n + 1)
                raw = res[:, n, :] if n < K else v_raw[n - K]
                nc.vector.scalar_tensor_tensor(out=win_lo[:, n // K, n % K, :], in0=raw,
                                               scalar=gamma_c[:, n % K:n % K + 1],
                                               in1=win_hi[:, n // K, n % K, :].bitcast(F32),
                                               op0=ALU.mult, op1=ALU.subtract).then_inc(piece_lo, 1)

            def biased(base, b, r):
                landed(base, count[0])
                for j, dst in enumerate((kb, vb)):
                    dve.wait_ge(kv_mm, b * (2 * R) + (2 * r + j + 1))
                    if r:
                        dve.wait_ge(squared, b * (2 * R) + (2 * (r - 1) + j + 1))
                        dve.wait_ge(crossed, b * R + r)
                        dve.wait_ge(prod_set, b * R + r)
                    nc.vector.tensor_tensor(dst[:], banks[2 * (r % 2) + j][:], bias_kv[:, j, :],
                                            ALU.add).then_inc(kv_biased, 1)

            def products(base, b, r):
                landed(base, count[0])
                dve.wait_ge(kv_biased, b * (2 * R) + (2 * r + 2))
                if r:
                    dve.wait_ge(turned_set, b * R + r)
                nc.vector.tensor_tensor(prod[:, 2:6, :].rearrange("p a i -> p (a i)"), kb, vb,
                                        ALU.mult).then_inc(prod_set, 1)

            def accumulate(base, b, r):
                dve.wait_ge(normed, b * R + (r + 1))
                y, t = nw[:, 0, :], nw[:, 1, :]
                link(base, nc.vector.reciprocal(y, nrm[:, r, :]))
                newton_rsqrt(base, y, nsq[:, r, :], t)
                link(base, nc.vector.tensor_tensor(wrow[:], nw[:, 0, 0:1], nw[:, 0, 1:2], ALU.mult))
                flat = "p a i -> p (a i)"

                def weighted(dst, src):
                    if r == 0:
                        return nc.vector.tensor_scalar(dst, src, wrow[:, 0:1], None, ALU.mult)
                    return nc.vector.scalar_tensor_tensor(out=dst, in0=src, scalar=wrow[:, 0:1], in1=dst,
                                                          op0=ALU.mult, op1=ALU.add)

                step(weighted(acc_p[:].rearrange(flat), prod[:, 2:6, :].rearrange(flat)))
                dve.wait_ge(turned_set, b * R + (r + 1))
                if r:
                    dve.wait_ge(summed, b * R + r)
                weighted(acc_r[:].rearrange(flat), turned[:].rearrange(flat)).then_inc(summed, 1)

            def combine(base, b):
                landed(base, count[0])
                dve.wait_ge(summed, b * R + R)
                step(nc.vector.tensor_tensor(prod[:, 0, :], acc_p[:, 0, :], acc_p[:, 1, :], ALU.add))
                step(nc.vector.tensor_tensor(prod[:, 1, :], acc_r[:, 2, :], acc_r[:, 3, :], ALU.subtract))
                link(base, nc.vector.tensor_tensor(prod[:, 2, :], acc_r[:, 0, :], acc_r[:, 1, :], ALU.add))
                link(base, nc.vector.tensor_tensor(prod[:, 3, :], prod[:, 1, :], prod[:, 2, :], ALU.subtract))
                nc.vector.tensor_tensor(acc_p[:, 0, :], prod[:, 0, :], prod[:, 3, :], ALU.add)
                nc.vector.tensor_tensor(acc_p[:, 1, :], prod[:, 0, :], prod[:, 3, :], ALU.subtract).then_inc(acc_set, 1)

            def attention_scale(b):
                dve.wait_ge(a_mm, b + 1)
                nc.vector.tensor_scalar(acol[:, 0, :], banks[7][:, 0:K], 0.5, None, ALU.add).then_inc(dve_step, 1)
                count[0] += 1

            def attention_bias(base):
                landed(base, count[0])
                nc.vector.tensor_tensor(acol[:, 1, :], acol[:, 0, :], bq_c[:], ALU.mult).then_inc(a_set, 1)

            def hidden_lo(b, c):
                dve.wait_ge(relu_set, b * H + (c + 1))
                nc.vector.tensor_tensor(hid_lo[:, c % HID_SLOTS, :], full[:, c % FULL_SLOTS, :],
                                        hid_hi[:, c % HID_SLOTS, :].bitcast(F32), ALU.subtract).then_inc(hid_set, 1)

            def residual(base, b, r):
                if r == 0:
                    dve.wait_ge(res_in, b * 16 + 16)
                link(base, nc.vector.tensor_scalar(res[:, r, :], res[:, r, :], cur[:, 0, r:r + 1], cur[:, 1, r:r + 1],
                                                   ALU.subtract, ALU.mult))
                step(nc.vector.tensor_tensor(res[:, r, :], res[:, r, :], bout_bc[:], ALU.add))

            def ffn_scaled(b, r):
                dve.wait_ge(down_mm, b * H + H)
                if r >= 2:
                    dve.wait_ge(res_set, b * R + (r - 1))
                nc.vector.scalar_tensor_tensor(out=(kb, vb)[r % 2], in0=banks[r][:], scalar=cur[:, 2, r:r + 1],
                                               in1=dscale_bc[:], op0=ALU.mult, op1=ALU.mult).then_inc(ffn_read, 1)

            def ffn_added(b, r):
                dve.wait_ge(ffn_read, b * R + (r + 1))
                nc.vector.scalar_tensor_tensor(out=res[:, r, :], in0=(kb, vb)[r % 2], scalar=cur[:, 0, r:r + 1],
                                               in1=res[:, r, :], op0=ALU.add, op1=ALU.add).then_inc(res_set, 1)

            def query_lo(b, q):
                dve.wait_ge(q_set, b * K + (q + 1))
                nc.vector.tensor_tensor(hid_lo[:, q, :], full[:, q % FULL_SLOTS, :], hid_hi[:, q, :].bitcast(F32),
                                        ALU.subtract).then_inc(q_split, 1)

            def finish(b, r):
                dve.wait_ge(y_mm, b * R + (r + 1))
                dve.wait_ge(res_set, b * R + (r + 1))
                nc.vector.tensor_tensor(res[:, r, :], banks[4 + r][:], res[:, r, :], ALU.add).then_inc(out_set, 1)

            def sequence(b, first, last, base):
                count[0] = 0
                step(nc.vector.tensor_copy(cur[:], nxt[:, 1:4, :]))
                for r in range(R):
                    if first and r == 1:
                        transposed_lo(2, banks[4])
                        transposed_lo(3, banks[5])
                    biased(base, b, r)
                    if r:
                        accumulate(base, b, r - 1)
                    products(base, b, r)
                for c in range(H):
                    hidden_lo(b, c)
                    if c == 0:
                        accumulate(base, b, R - 1)
                    if c == 1:
                        combine(base, b)
                    if c == 2 and first:
                        dve.wait_ge(bias_q_mm, 1)
                        nc.vector.tensor_tensor(bq_c[:], banks[7][:, 8:8 + K], bq_c[:], ALU.add).then_inc(bq_set, 1)
                    if c == 3:
                        if first:
                            dve.wait_ge(bq_set, 1)
                        attention_scale(b)
                        attention_bias(base)
                    if not last:
                        if 4 <= c < 4 + R:
                            if c == 4:
                                dve.wait_ge(x_rows_in, b * (16 * R) + 16 * R)
                            step(row_stats(c - 4, x_rows[c - 4]))
                        if c == 4 + R:
                            landed(base, count[0])
                            moments(base, slice(0, R))
                        if c == 5 + R:
                            scales(base, b + 3, slice(0, R))
                            nc.vector.tensor_copy(nxt[:, 0, :], inv[:, 1, :]).then_inc(stats_set, 1)
                        if c >= H - K:
                            normalise_cols(base, b, c - (H - K))
                    if c == H - R and first:
                        dve.wait_ge(scales_in, 3 * 16)
                        link(base, nc.vector.tensor_scalar(dscale_bc[:], dscale_bc[:], oscale_c[:, 0:1], None, ALU.mult))
                    at = H - R if first else H - 2 * R
                    if at <= c < at + R:
                        residual(base, b, c - at)
                if not last:
                    dve.wait_ge(z_set, b * K + 2 * K)
                landed(base, count[0])
                ffn_scaled(b, 0)
                ffn_scaled(b, 1)
                ffn_added(b, 0)
                ffn_added(b, 1)
                query_lo(b, 0)
                ffn_scaled(b, 2)
                ffn_scaled(b, 3)
                ffn_added(b, 2)
                ffn_added(b, 3)
                query_lo(b, 1)
                query_lo(b, 2)
                query_lo(b, 3)
                if not last:
                    for k in range(K):
                        split_lo(b + 1, k)
                for r in range(R):
                    finish(b, r)
                return count[0]

            def first_stats(half):
                for r in half:
                    dve.wait_ge(x0_in[r], 16)
                    step(row_stats(r, xz[:, r, :]))
                landed(0, count[0])
                moments(0, slice(half[0], half[-1] + 1))

            first_stats((0, 1))
            piece(0)
            scales(0, 1, slice(0, 2))
            normalise(0)
            normalise(1)
            piece(1)
            piece(2)
            transposed_lo(0, banks[4])
            piece(3)
            transposed_lo(1, banks[5])
            for n in range(K, 2 * K):
                piece(n)
            first_stats((2, 3))
            scales(0, 2, slice(2, R))
            normalise(2)
            normalise(3)
            landed(0, count[0])
            dve.wait_ge(tables_in, 4 * 16)
            for j in range(2):
                dve.wait_ge(*((beta_mm, K), (beta_v_mm, 1))[j])
                nc.vector.tensor_tensor(bias_kv[:, j, :], banks[6 + j][:], bias_kv[:, j, :], ALU.add).then_inc(bias_kv_set, 1)
            dve.wait_ge(bias_kv_set, 2)
            dve.wait_ge(piece_lo, 2 * K)
            start = count[0]
            n0 = sequence(0, True, False, start)
            per = n0 - 1
            with dve.Fori(1, LAST) as b:
                assert sequence(b, False, False, b * per + (start + 1)) == per
            sequence(LAST, False, True, LAST * per + (start + 1))

        @block.tensor
        def _(pe):
            mm = nc.tensor.matmul

            def three_pass(dst, l_hi, l_lo, r_hi, r_lo, k):
                mm(dst, l_hi, r_hi, start=(k == 0), stop=False)
                mm(dst, l_lo, r_hi, start=False, stop=False)
                return mm(dst, l_hi, r_lo, start=False, stop=(k == K - 1))

            def transposes(r, bank):
                for k in range(K):
                    last = nc.tensor.transpose(bank[:, k * P:(k + 1) * P], xz[:, r, k * P:(k + 1) * P], ident[:])
                last.then_inc(t_mm, 1)

            def beta_key(n):
                pe.wait_ge(piece_in[n], 16)
                pe.wait_ge(consts_set, 4 + (n + 1))
                last = mm(banks[6][:], beta_bc[:, n, :], res[:, n, :], start=(n == 0), stop=(n == K - 1))
                last.then_inc(beta_mm, 1)

            def beta_value():
                pe.wait_ge(beta_summed, K)
                mm(banks[7][:], ones, beta_sum[0], start=True, stop=True).then_inc(beta_v_mm, 1)

            def bias_query():
                pe.wait_ge(beta_summed, 2 * K)
                pe.wait_ge(bias_kv_set, 2)
                for q in range(K):
                    last = mm(banks[7][:, 8 + q:9 + q], beta_sum[1][:, q * P:(q + 1) * P], half_c[:, 2:3],
                              start=True, stop=True)
                last.then_inc(bias_q_mm, 1)

            def keys_values(b, r, first):
                s = slice(r * P, (r + 1) * P)
                if first:
                    pe.wait_ge(zt_set, r + 1)
                elif r == 0:
                    pe.wait_ge(zt_set, b * K + K)
                    pe.wait_ge(ffn_read, b * R)
                for j in range(2):
                    if r >= 2:
                        pe.wait_ge(kv_biased, b * (2 * R) + (2 * (r - 2) + j + 1))
                    for k in range(K):
                        if first and r == 0:
                            pe.wait_ge(piece_lo, j * K + (k + 1))
                        last = three_pass(banks[2 * (r % 2) + j][:], zt_hi[:, k, s], zt_lo[:, k, s],
                                          win_hi[:, j, k, :], win_lo[:, j, k, :], k)
                    last.then_inc(kv_mm, 1)
                    if first and r == 0 and j == 1:
                        beta_value()
                    if first and r == 1 and j == 0:
                        for t in (2, 3):
                            pe.wait_ge(z_set, t + 1)
                            pe.wait_ge(zt_set, t - 1)
                            transposes(t, banks[2 + t])

            def up_proj(b, c, first):
                bank = banks[4 + c % UP_BANKS]
                if c >= UP_BANKS:
                    pe.wait_ge(relu_set, b * H + (c - UP_BANKS + 1))
                if first:
                    pe.wait_ge(up_signed, c + 1)
                for k in range(K):
                    mm(bank[:], up_sign[:, c, k, :], zt_hi[:, k, :], start=(k == 0), stop=False)
                    last = mm(bank[:], up_sign[:, c, k, :], zt_lo[:, k, :], start=False, stop=(k == K - 1))
                last.then_inc(up_mm, 1)

            def down_proj(b, c, first):
                pe.wait_ge(hid_set, b * H + (c + 1))
                if first:
                    pe.wait_ge(down_signed, c + 1)
                for r in range(R):
                    s = slice(r * P, (r + 1) * P)
                    mm(banks[r][:], hid_hi[:, c % HID_SLOTS, s], down_sign[:, c, :], start=(c == 0), stop=False)
                    last = mm(banks[r][:], hid_lo[:, c % HID_SLOTS, s], down_sign[:, c, :], start=False,
                              stop=(c == H - 1))
                last.then_inc(down_mm, 1)

            def row_sums(b):
                pe.wait_ge(acc_set, b + 1)
                for q in range(K):
                    last = mm(banks[7][:, q:q + 1], acc_p[:, q, :], half_c[:, q // 2:q // 2 + 1], start=True, stop=True)
                last.then_inc(a_mm, 1)

            def sequence(b, first, last):
                for r in range(R):
                    keys_values(b, r, first)
                if first:
                    pe.wait_ge(bias_kv_set, 2)
                else:
                    pe.wait_ge(out_set, b * R)
                for c in range(H + DOWN_LAG):
                    if c < H:
                        up_proj(b, c, first)
                    if c == DOWN_LAG:
                        pe.wait_ge(kv_biased, b * (2 * R) + 2 * R)
                    if c >= DOWN_LAG:
                        down_proj(b, c - DOWN_LAG, first)
                    if c == 3 and first:
                        bias_query()
                    if c == 4:
                        if first:
                            pe.wait_ge(bq_set, 1)
                        row_sums(b)
                pe.wait_ge(relu_set, b * H + H)
                pe.wait_ge(a_set, b + 1)
                if first:
                    pe.wait_ge(wq_set, K)
                for q in range(K):
                    s = slice(q * P, (q + 1) * P)
                    for k in range(K):
                        done = three_pass(banks[4 + q][:], win_hi[:, 2, k, s], win_lo[:, 2, k, s], zt_hi[:, k, :],
                                          zt_lo[:, k, :], k)
                    done.then_inc(q_mm, 1)
                if first:
                    pe.wait_ge(wout_set, K)
                together = [(r, k) for ks in (range(K - 1), range(K - 1, K)) for r in range(2) for k in ks]
                for r, k in together + [(r, k) for r in range(2, R) for k in range(K)]:
                    s = slice(r * P, (r + 1) * P)
                    if r == 0:
                        pe.wait_ge(q_split, b * K + (k + 1))
                    done = three_pass(banks[4 + r][:], hid_hi[:, k, s], hid_lo[:, k, s], wout_hi[:, k, :],
                                      wout_lo[:, k, :], k)
                    if k == K - 1:
                        done.then_inc(y_mm, 1)

            pe.wait_ge(gains_in, 3 * 16)
            beta_key(0)
            beta_key(1)
            for r in range(2):
                pe.wait_ge(z_set, r + 1)
                transposes(r, banks[4 + r])
            beta_key(2)
            beta_key(3)
            sequence(0, True, False)
            with pe.Fori(1, LAST) as b:
                sequence(b, False, False)
            sequence(LAST, False, True)


def kernel(**inputs):
    import numpy as _np
    import concourse.bacc as _bacc
    from concourse import mybir as _mybir
    from concourse.bass_utils import run_bass_kernel_spmd as _run

    x = _np.asarray(inputs["L0_attn_X"])
    n_seq, seq, d = x.shape
    rot_dim, k = d // 2, d // P
    order = _np.concatenate([_np.arange(0, rot_dim, 2), _np.arange(1, rot_dim, 2), _np.arange(rot_dim, d)])
    w_in = _np.asarray(inputs["L0_attn_W_in"])
    b_in = _np.asarray(inputs["L0_attn_b_in"])
    q_cols, k_cols, v_cols = order, order + d, order + 2 * d
    up = _np.asarray(inputs["L0_ffn_up_weight"])
    down = _np.asarray(inputs["L0_ffn_down_weight"])
    h = up.shape[0] // P

    def columns(v):
        return v.reshape(-1, P).T

    inv_freq = (_np.float32(1.0) / _np.float32(THETA) ** (_np.arange(0, rot_dim, 2, dtype=_np.float32)
                                                        / _np.float32(rot_dim))).astype(_np.float32)
    angle = (_np.arange(seq, dtype=_np.float32)[:, None] * inv_freq[None, :]).astype(_np.float32).astype(_np.float64)
    rotation = _np.stack([_np.sin(2 * angle), _np.cos(2 * angle)], axis=1).astype(_np.float32)

    arrays = {
        "x": x,
        "x_cols": x.transpose(0, 2, 1).reshape(n_seq, k, P, seq),
        "w_in": _np.stack([w_in[:, c].reshape(k, P, d) for c in (k_cols, v_cols, q_cols)]),
        "w_out": _np.asarray(inputs["L0_attn_W_out"])[order].reshape(k, P, d),
        "up": up.reshape(h, P, k, P).transpose(0, 3, 2, 1).reshape(h, P, k * P),
        "down": down.T.reshape(h, P, d),
        "gamma": columns(_np.asarray(inputs["L0_attn_gamma"])),
        "beta": columns(_np.asarray(inputs["L0_attn_beta"])),
        "b_kv": _np.concatenate([b_in[k_cols], b_in[v_cols]]),
        "b_q": columns(b_in[q_cols]),
        "b_out": _np.asarray(inputs["L0_attn_b_out"]),
        "up_scale": columns(_np.asarray(inputs["L0_ffn_up_scale"])),
        "down_scale": _np.asarray(inputs["L0_ffn_down_scale"]),
        "output_scale": _np.asarray(inputs["L0_ffn_output_scale"]),
        "rotation": rotation.reshape(seq // P, P, 2, rot_dim // 2).transpose(1, 0, 2, 3),
        "identity": _np.eye(P, dtype=_np.float32),
    }
    nc = _bacc.Bacc("TRN2", target_bir_lowering=False, num_devices=1)
    feeds, args = {}, []
    for name, a in arrays.items():
        feeds[f"in_{name}"] = _np.ascontiguousarray(a)
        args.append(nc.dram_tensor(f"in_{name}", a.shape, _mybir.dt.from_np(a.dtype), kind="ExternalInput").ap())
    args.append(nc.dram_tensor("row_scales", (n_seq, P, 2, seq // P), _mybir.dt.float32, kind="Internal").ap())
    args.append(nc.dram_tensor("out_0", x.shape, _mybir.dt.float32, kind="ExternalOutput").ap())
    attention_ffn_kernel(nc, *args)
    r = _run(nc, [feeds], core_ids=[0])
    return r.results[0]["out_0"]
```
